# Optimizing a Trainium2 kernel written in Bass

```python
import numpy as np
import jax
import jax.numpy as jnp

def _softmax(x, axis=-1):
    return jax.nn.softmax(x, axis=axis)

def _gelu(x):
    return jax.nn.gelu(x, approximate=True)

def _silu(x):
    return jax.nn.silu(x)

def _sigmoid(x):
    return jax.nn.sigmoid(x)

def _layernorm(x, axis=-1, eps=1e-05):
    m = jnp.mean(x, axis=axis, keepdims=True)
    v = jnp.var(x, axis=axis, keepdims=True)
    return (x - m) / jnp.sqrt(v + eps)

def _scatter_add(tgt, idx, src, axis=0):
    return tgt.at[idx].add(src)

def _segment_sum(src, seg, n):
    return jax.ops.segment_sum(src, seg, n)
kernel_name = 'mk_xattn_ffn_d2_seqx_r8_085b92'

def setup_inputs(seed: int=0):
    np.random.seed(seed)
    _w = jnp.asarray

    def _rec_inputs():
        import jax
        import jax.numpy as jnp
        _rk = jax.random.key(seed)
        x = -0.000125 + 0.9999 * jax.random.normal(jax.random.fold_in(_rk, 1), (4, 256, 256), jnp.float32)
        _lenS = 256 - jax.random.randint(jax.random.fold_in(_rk, 7), (4,), 0, max(1, 256 // 4) + 1, jnp.int32)
        _lenS2 = 1601 - jax.random.randint(jax.random.fold_in(_rk, 8), (4,), 0, max(1, 1601 // 4) + 1, jnp.int32)
        _ctx_2048P = jax.random.normal(jax.random.fold_in(_rk, 11), (4, 16, 256), jnp.float32)
        _ctx_2048c = jax.random.dirichlet(jax.random.fold_in(_rk, 511), 0.3 * jnp.ones((16,), jnp.float32), (4, 1601))
        _ctx_2048t = jnp.einsum('bsk,bkd->bsd', _ctx_2048c, _ctx_2048P)
        _ctx_2048t = _ctx_2048t * jax.lax.rsqrt(jnp.mean(jnp.square(_ctx_2048t)) + 1e-12) * 0.953939
        ctx_2048 = -0.000514642 + 1.00011 * (_ctx_2048t + 0.3 * jax.random.normal(jax.random.fold_in(_rk, 611), (4, 1601, 256), jnp.float32))
        _validS = jnp.arange(256)[None, :] < _lenS[:, None]
        _validS2 = jnp.arange(1601)[None, :] < _lenS2[:, None]
        _causal = jnp.tril(jnp.ones((256, 256), dtype=bool))
        mask_BxS2_bk0 = jnp.logical_not(jnp.broadcast_to(_validS2[:, :], (4, 1601)))
        mask_BxS2_ik0 = jnp.where(jnp.broadcast_to(_validS2[:, :], (4, 1601)), 0, 1).astype(jnp.int32)
        return (x, ctx_2048, mask_BxS2_bk0, mask_BxS2_ik0)
    x, ctx_2048, mask_BxS2_bk0, mask_BxS2_ik0 = _rec_inputs()

    def _L0_xattn_setup():
        import jax, jax.numpy as jnp
        import numpy as np
        key = jax.random.key(seed)
        k1, k2, k3 = jax.random.split(key, 3)
        B, S, D, M = (8, 256, 256, 128)
        hidden_states = jax.random.normal(k1, (B, S, D), dtype=jnp.float32)
        memory_tokens = jax.random.normal(k2, (B, M, D), dtype=jnp.float32)
        memory_mask = jax.random.randint(k3, (B, M), 0, 2).astype(jnp.bool_)
        return {'hidden_states': hidden_states, 'memory_tokens': memory_tokens, 'memory_mask': memory_mask}
    _L0_xattn_all = _L0_xattn_setup()
    _L0_xattn_in = {k: v for k, v in _L0_xattn_all.items() if k in ()}
    del _L0_xattn_all

    def _L0_ffn_setup():
        import jax, jax.numpy as jnp
        import numpy as np
        H = 256
        I = 176
        E = 16
        G = 4
        TOPK_GROUP = 2
        TOP_K = 6
        N_SHARED = 2
        SCALE_FACTOR = 2.5
        B, S = (2, 256)

        def _gate(hs_flat, gate_weight, bias):
            T = hs_flat.shape[0]
            logits = hs_flat @ gate_weight.T
            scores = jax.nn.sigmoid(logits)
            scores_for_choice = scores + bias[None, :]
            gs = scores_for_choice.reshape(T, G, E // G)
            group_scores = jnp.sum(jax.lax.top_k(gs, 2)[0], axis=-1)
            _, group_idx = jax.lax.top_k(group_scores, TOPK_GROUP)
            group_mask = jnp.zeros((T, G), scores.dtype).at[jnp.arange(T)[:, None], group_idx].set(1.0)
            score_mask = jnp.repeat(group_mask, E // G, axis=1)
            tmp_scores = jnp.where(score_mask > 0, scores_for_choice, 0.0)
            _, topk_idx = jax.lax.top_k(tmp_scores, TOP_K)
            topk_weight = jnp.take_along_axis(scores, topk_idx, axis=1)
            topk_weight = topk_weight / (jnp.sum(topk_weight, axis=-1, keepdims=True) + 1e-20)
            topk_weight = topk_weight * SCALE_FACTOR
            return (topk_idx, topk_weight)
        key = jax.random.key(seed)
        ks = jax.random.split(key, 8)
        scale = 0.01
        SI = I * N_SHARED
        return {'hidden_states': jax.random.normal(ks[0], (B, S, H), jnp.float32), 'gate_weight': jax.random.uniform(ks[1], (E, H), jnp.float32, -0.05, 0.05), 'e_score_correction_bias': jnp.zeros((E,), jnp.float32), 'gate_proj': jax.random.normal(ks[2], (E, I, H), jnp.float32) * scale, 'up_proj': jax.random.normal(ks[3], (E, I, H), jnp.float32) * scale, 'down_proj': jax.random.normal(ks[4], (E, H, I), jnp.float32) * scale, 'shared_gate_w': jax.random.normal(ks[5], (SI, H), jnp.float32) * scale, 'shared_up_w': jax.random.normal(ks[6], (SI, H), jnp.float32) * scale, 'shared_down_w': jax.random.normal(ks[7], (H, SI), jnp.float32) * scale}
    _L0_ffn_all = _L0_ffn_setup()
    _L0_ffn_in = {k: v for k, v in _L0_ffn_all.items() if k in ('gate_weight', 'e_score_correction_bias', 'gate_proj', 'up_proj', 'down_proj', 'shared_gate_w', 'shared_up_w', 'shared_down_w')}
    del _L0_ffn_all

    def _L1_xattn_setup():
        import jax, jax.numpy as jnp
        import numpy as np
        import math
        H = 256
        NH = 16
        HD = H // NH
        EPS_LN = 1e-05
        RES_SCALE_MAX = 0.3

        def _nan_clean(x, lim=10000.0):
            return jnp.nan_to_num(x, nan=0.0, posinf=lim, neginf=-lim)
        key = jax.random.key(seed)
        ks = jax.random.split(key, 12)
        B, S, T = (4, 256, 32)
        std = 1.0 / math.sqrt(H)
        return {'hidden_states': jax.random.normal(ks[0], (B, S, H), jnp.float32), 'audio_tokens': jax.random.normal(ks[1], (B, T, H), jnp.float32), 'attention_mask': jax.random.randint(ks[2], (B, T), 0, 2, jnp.int32), 'Wq': jax.random.normal(ks[3], (H, H), jnp.float32) * std, 'bq': jnp.zeros((H,), jnp.float32), 'Wk': jax.random.normal(ks[4], (H, H), jnp.float32) * std, 'bk': jnp.zeros((H,), jnp.float32), 'Wv': jax.random.normal(ks[5], (H, H), jnp.float32) * std, 'bv': jnp.zeros((H,), jnp.float32), 'Wo': jax.random.normal(ks[6], (H, H), jnp.float32) * std, 'bo': jnp.zeros((H,), jnp.float32), 'ln_gamma': jnp.ones((H,), jnp.float32), 'ln_beta': jnp.zeros((H,), jnp.float32), 'residual_scale': jnp.float32(0.05)}
    _L1_xattn_all = _L1_xattn_setup()
    _L1_xattn_in = {k: v for k, v in _L1_xattn_all.items() if k in ('Wq', 'bq', 'Wk', 'bk', 'Wv', 'bv', 'Wo', 'bo', 'ln_gamma', 'ln_beta', 'residual_scale')}
    del _L1_xattn_all

    def _L1_ffn_setup():
        import jax, jax.numpy as jnp
        import numpy as np
        DIM = 256
        EXPERT_DIM = 128
        N_EXPERTS = 16
        TOPK = 2
        N_SHARED = 1
        B, T = (4, 256)
        key = jax.random.key(seed)
        ks = jax.random.split(key, 9)
        s = 0.02
        return {'x': jax.random.normal(ks[0], (B, T, DIM), jnp.float32), 'router_w': jax.random.normal(ks[1], (N_EXPERTS, DIM), jnp.float32) * s, 'router_bias': jnp.zeros((N_EXPERTS,), jnp.float32), 'Wu': jax.random.normal(ks[2], (N_EXPERTS, DIM, EXPERT_DIM), jnp.float32) * s, 'Wg': jax.random.normal(ks[3], (N_EXPERTS, DIM, EXPERT_DIM), jnp.float32) * s, 'Wd': jax.random.normal(ks[4], (N_EXPERTS, EXPERT_DIM, DIM), jnp.float32) * s, 'Su': jax.random.normal(ks[5], (N_SHARED, DIM, EXPERT_DIM * TOPK), jnp.float32) * s, 'Sg': jax.random.normal(ks[6], (N_SHARED, DIM, EXPERT_DIM * TOPK), jnp.float32) * s, 'Sd': jax.random.normal(ks[7], (N_SHARED, EXPERT_DIM * TOPK, DIM), jnp.float32) * s}
    _L1_ffn_all = _L1_ffn_setup()
    _L1_ffn_in = {k: v for k, v in _L1_ffn_all.items() if k in ('router_w', 'router_bias', 'Wu', 'Wg', 'Wd', 'Su', 'Sg', 'Sd')}
    del _L1_ffn_all
    return {'x': x, 'ctx_2048': ctx_2048, 'mask_BxS2_bk0': mask_BxS2_bk0, 'mask_BxS2_ik0': mask_BxS2_ik0, 'L0_ffn_gate_weight': _L0_ffn_in['gate_weight'], 'L0_ffn_e_score_correction_bias': _L0_ffn_in['e_score_correction_bias'], 'L0_ffn_gate_proj': _L0_ffn_in['gate_proj'], 'L0_ffn_up_proj': _L0_ffn_in['up_proj'], 'L0_ffn_down_proj': _L0_ffn_in['down_proj'], 'L0_ffn_shared_gate_w': _L0_ffn_in['shared_gate_w'], 'L0_ffn_shared_up_w': _L0_ffn_in['shared_up_w'], 'L0_ffn_shared_down_w': _L0_ffn_in['shared_down_w'], 'L1_xattn_Wq': _L1_xattn_in['Wq'], 'L1_xattn_bq': _L1_xattn_in['bq'], 'L1_xattn_Wk': _L1_xattn_in['Wk'], 'L1_xattn_bk': _L1_xattn_in['bk'], 'L1_xattn_Wv': _L1_xattn_in['Wv'], 'L1_xattn_bv': _L1_xattn_in['bv'], 'L1_xattn_Wo': _L1_xattn_in['Wo'], 'L1_xattn_bo': _L1_xattn_in['bo'], 'L1_xattn_ln_gamma': _L1_xattn_in['ln_gamma'], 'L1_xattn_ln_beta': _L1_xattn_in['ln_beta'], 'L1_xattn_residual_scale': _L1_xattn_in['residual_scale'], 'L1_ffn_router_w': _L1_ffn_in['router_w'], 'L1_ffn_router_bias': _L1_ffn_in['router_bias'], 'L1_ffn_Wu': _L1_ffn_in['Wu'], 'L1_ffn_Wg': _L1_ffn_in['Wg'], 'L1_ffn_Wd': _L1_ffn_in['Wd'], 'L1_ffn_Su': _L1_ffn_in['Su'], 'L1_ffn_Sg': _L1_ffn_in['Sg'], 'L1_ffn_Sd': _L1_ffn_in['Sd']}

def reference(x, ctx_2048, mask_BxS2_bk0, mask_BxS2_ik0, L0_ffn_gate_weight, L0_ffn_e_score_correction_bias, L0_ffn_gate_proj, L0_ffn_up_proj, L0_ffn_down_proj, L0_ffn_shared_gate_w, L0_ffn_shared_up_w, L0_ffn_shared_down_w, L1_xattn_Wq, L1_xattn_bq, L1_xattn_Wk, L1_xattn_bk, L1_xattn_Wv, L1_xattn_bv, L1_xattn_Wo, L1_xattn_bo, L1_xattn_ln_gamma, L1_xattn_ln_beta, L1_xattn_residual_scale, L1_ffn_router_w, L1_ffn_router_bias, L1_ffn_Wu, L1_ffn_Wg, L1_ffn_Wd, L1_ffn_Su, L1_ffn_Sg, L1_ffn_Sd):
    import jax
    import jax.numpy as jnp

    def _L0_xattn_ref(hidden_states, memory_tokens, memory_mask):
        import jax, jax.numpy as jnp
        import numpy as np
        B, S, D = hidden_states.shape
        scale = 1.0 / jnp.sqrt(jnp.asarray(D, hidden_states.dtype))
        scores = jnp.einsum('bsd,bmd->bsm', hidden_states, memory_tokens) * scale
        neg_inf = jnp.asarray(-1e+30, scores.dtype)
        scores = jnp.where(memory_mask[:, None, :], scores, neg_inf)
        attn = jax.nn.softmax(scores, axis=-1)
        readout = jnp.einsum('bsm,bmd->bsd', attn, memory_tokens)
        valid_b = jnp.any(memory_mask, axis=-1)
        out = jnp.where(valid_b[:, None, None], readout, jnp.zeros_like(readout))
        return out

    def _L0_ffn_ref(hidden_states, gate_weight, e_score_correction_bias, gate_proj, up_proj, down_proj, shared_gate_w, shared_up_w, shared_down_w):
        import jax, jax.numpy as jnp
        import numpy as np
        H = 256
        I = 176
        E = 16
        G = 4
        TOPK_GROUP = 2
        TOP_K = 6
        N_SHARED = 2
        SCALE_FACTOR = 2.5
        B, S = (2, 256)

        def _gate(hs_flat, gate_weight, bias):
            T = hs_flat.shape[0]
            logits = hs_flat @ gate_weight.T
            scores = jax.nn.sigmoid(logits)
            scores_for_choice = scores + bias[None, :]
            gs = scores_for_choice.reshape(T, G, E // G)
            group_scores = jnp.sum(jax.lax.top_k(gs, 2)[0], axis=-1)
            _, group_idx = jax.lax.top_k(group_scores, TOPK_GROUP)
            group_mask = jnp.zeros((T, G), scores.dtype).at[jnp.arange(T)[:, None], group_idx].set(1.0)
            score_mask = jnp.repeat(group_mask, E // G, axis=1)
            tmp_scores = jnp.where(score_mask > 0, scores_for_choice, 0.0)
            _, topk_idx = jax.lax.top_k(tmp_scores, TOP_K)
            topk_weight = jnp.take_along_axis(scores, topk_idx, axis=1)
            topk_weight = topk_weight / (jnp.sum(topk_weight, axis=-1, keepdims=True) + 1e-20)
            topk_weight = topk_weight * SCALE_FACTOR
            return (topk_idx, topk_weight)
        b, s, h = hidden_states.shape
        hs = hidden_states.reshape(-1, h)
        T = hs.shape[0]
        topk_idx, topk_weight = _gate(hs, gate_weight, e_score_correction_bias)
        comb = jnp.zeros((T, E), hs.dtype).at[jnp.arange(T)[:, None], topk_idx].add(topk_weight)
        out = jnp.zeros_like(hs)
        for e in range(E):
            g = hs @ gate_proj[e].T
            u = hs @ up_proj[e].T
            inter = jax.nn.silu(g) * u
            out = out + comb[:, e:e + 1] * (inter @ down_proj[e].T)
        y = out.reshape(b, s, h)
        sg = hidden_states @ shared_gate_w.T
        su = hidden_states @ shared_up_w.T
        shared_out = jax.nn.silu(sg) * su @ shared_down_w.T
        return y + shared_out

    def _L1_xattn_ref(hidden_states, audio_tokens, attention_mask, Wq, bq, Wk, bk, Wv, bv, Wo, bo, ln_gamma, ln_beta, residual_scale):
        import jax, jax.numpy as jnp
        import numpy as np
        import math
        H = 256
        NH = 16
        HD = H // NH
        EPS_LN = 1e-05
        RES_SCALE_MAX = 0.3

        def _nan_clean(x, lim=10000.0):
            return jnp.nan_to_num(x, nan=0.0, posinf=lim, neginf=-lim)
        B, S, _ = hidden_states.shape
        T = audio_tokens.shape[1]
        hs = _nan_clean(hidden_states).astype(jnp.float32)
        at = _nan_clean(audio_tokens).astype(jnp.float32)

        def proj(x, W, b, L):
            y = x @ W.T + b
            return y.reshape(B, L, NH, HD).transpose(0, 2, 1, 3)
        q = _nan_clean(proj(hs, Wq, bq, S))
        k = _nan_clean(proj(at, Wk, bk, T))
        v = _nan_clean(proj(at, Wv, bv, T))
        scale = max(math.sqrt(HD), 1e-08)
        scores = jnp.einsum('bhsd,bhtd->bhst', q, k) / scale
        scores = jnp.clip(scores, -50.0, 50.0)
        scores = jnp.nan_to_num(scores, nan=0.0, posinf=50.0, neginf=-50.0)
        attend = (attention_mask.astype(jnp.float32) > 0.5)[:, None, None, :]
        scores = jnp.where(attend, scores, -10000.0)
        scores = jnp.clip(scores, -50.0, 50.0)
        probs = jax.nn.softmax(scores, axis=-1)
        probs = jnp.nan_to_num(probs, nan=0.0, posinf=1.0, neginf=0.0)
        probs = probs / (probs.sum(axis=-1, keepdims=True) + 1e-08)
        ctx = jnp.einsum('bhst,bhtd->bhsd', probs, v)
        ctx = ctx.transpose(0, 2, 1, 3).reshape(B, S, H)
        delta = _nan_clean(ctx @ Wo.T + bo)
        rs = jnp.clip(residual_scale, 0.0, RES_SCALE_MAX)
        delta = rs * delta
        mu = delta.mean(axis=-1, keepdims=True)
        var = jnp.mean((delta - mu) ** 2, axis=-1, keepdims=True)
        delta = (delta - mu) / jnp.sqrt(var + EPS_LN) * ln_gamma + ln_beta
        return delta

    def _L1_ffn_ref(x, router_w, router_bias, Wu, Wg, Wd, Su, Sg, Sd):
        import jax, jax.numpy as jnp
        import numpy as np
        DIM = 256
        EXPERT_DIM = 128
        N_EXPERTS = 16
        TOPK = 2
        N_SHARED = 1
        B, T = (4, 256)
        Bx, Tx, D = x.shape
        flat = x.reshape(Bx * Tx, D)
        logits = flat @ router_w.T
        scores = jax.nn.softmax(logits, axis=-1)
        _, topk_idx = jax.lax.top_k(logits + router_bias, TOPK)
        topk_scores = jnp.take_along_axis(scores, topk_idx, axis=-1)
        topk_scores = topk_scores / topk_scores.sum(-1, keepdims=True)
        combine = jnp.einsum('nk,nke->ne', topk_scores, jax.nn.one_hot(topk_idx, N_EXPERTS, dtype=scores.dtype))
        out = jnp.zeros_like(flat)
        for e in range(N_EXPERTS):
            h = jax.nn.silu(flat @ Wu[e]) * (flat @ Wg[e])
            out = out + combine[:, e:e + 1] * (h @ Wd[e])
        for s in range(N_SHARED):
            out = out + jax.nn.silu(flat @ Su[s]) * (flat @ Sg[s]) @ Sd[s]
        return out.reshape(Bx, Tx, D)
    x = x + _L0_xattn_ref(_layernorm(x, axis=-1), ctx_2048, mask_BxS2_bk0)
    x = x + _L0_ffn_ref(_layernorm(x, axis=-1), L0_ffn_gate_weight, L0_ffn_e_score_correction_bias, L0_ffn_gate_proj, L0_ffn_up_proj, L0_ffn_down_proj, L0_ffn_shared_gate_w, L0_ffn_shared_up_w, L0_ffn_shared_down_w)
    x = x + _L1_xattn_ref(_layernorm(x, axis=-1), ctx_2048, mask_BxS2_ik0, L1_xattn_Wq, L1_xattn_bq, L1_xattn_Wk, L1_xattn_bk, L1_xattn_Wv, L1_xattn_bv, L1_xattn_Wo, L1_xattn_bo, L1_xattn_ln_gamma, L1_xattn_ln_beta, L1_xattn_residual_scale)
    x = x + _L1_ffn_ref(_layernorm(x, axis=-1), L1_ffn_router_w, L1_ffn_router_bias, L1_ffn_Wu, L1_ffn_Wg, L1_ffn_Wd, L1_ffn_Su, L1_ffn_Sg, L1_ffn_Sd)
    return x

_drawn_inputs = setup_inputs


def setup_inputs(seed=0):
    import zlib

    import numpy as np

    out = dict(_drawn_inputs(seed))
    spreads = {'L0_ffn_e_score_correction_bias': (0.0, 0.8),
     'L1_xattn_bq': (0.0, 0.321),
     'L1_xattn_bk': (0.0, 0.8),
     'L1_xattn_bv': (0.0, 0.1),
     'L1_xattn_bo': (0.0, 0.1),
     'L1_xattn_ln_gamma': (1.0, 0.2),
     'L1_xattn_ln_beta': (0.0, 0.1),
     'L1_ffn_router_bias': (0.0, 0.8)}
    factors = {'L0_ffn_gate_weight': 8.0,
     'L0_ffn_gate_proj': 8.0,
     'L0_ffn_up_proj': 8.0,
     'L0_ffn_down_proj': 8.0,
     'L0_ffn_shared_gate_w': 8.0,
     'L0_ffn_shared_up_w': 8.0,
     'L0_ffn_shared_down_w': 8.0,
     'L1_ffn_router_w': 8.0,
     'L1_ffn_Wu': 8.0,
     'L1_ffn_Wg': 8.0,
     'L1_ffn_Wd': 8.0,
     'L1_ffn_Su': 4.409,
     'L1_ffn_Sg': 4.685,
     'L1_ffn_Sd': 4.412}
    for name, (base, spread) in spreads.items():
        noise = np.random.default_rng([zlib.crc32(name.encode()), seed]).standard_normal(out[name].shape)
        drawn = base * np.exp(spread * noise) if base else spread * noise
        out[name] = jnp.asarray(drawn.astype(out[name].dtype))
    for name, factor in factors.items():
        out[name] = (out[name] * factor).astype(out[name].dtype)
    return out
```

```python
from contextlib import ExitStack

import numpy as np
import concourse.bass as bass
from concourse import mybir

F32 = mybir.dt.float32
F32R = mybir.dt.float32r
U8 = mybir.dt.uint8
I32 = mybir.dt.int32
ALU = mybir.AluOpType
ACT = mybir.ActivationFunctionType
AX = mybir.AxisListType

P = 128
NB, SEQ, D = 4, 256, 256
NT = NB * SEQ // P
KT = D // P
M = 1601
MP = M + M % 2
MW = -(-M // 4)
MT = -(-M // P)
TAIL = M - (MT - 1) * P
MCH = [(c * 512, min(512, MP - c * 512)) for c in range(-(-MP // 512))]
NH, HD = 16, 16
NPAIR = NH // 2
PR = 2 * HD
NJ = NB * NPAIR
VC = 2 * PR + 1
QROWS = 3 * PR + 1
E = 16
I0, SH0 = 176, 352
I1, SH1 = 128, 256
NSH0 = -(-SH0 // P)
NEX0 = E * I0 // P
NSH1 = SH1 // P
NEX1 = E * I1 // P
WC = 3 * D + P
EPS = 1e-5
CLO, CHI = float(np.exp(-50.0)), float(np.exp(50.0))
VUNITS = [(0, 2), (2, 2), (4, 2), (6, 2), (8, 2), (10, 1), (11, 1), (12, 1)]
PIECES = [("t", 0, 0, 1024), ("t", 1, 0, 1024), ("t", 0, 1024, MP - 1024), ("t", 1, 1024, MP - 1024),
          ("n", 0, 0, 4), ("n", 0, 4, 4), ("n", 0, 8, 4), ("n", 0, 12, 1)]
NP_ = len(PIECES)
NCH = 7
PSLOT = [0, 1, 2, 3, 0, 1, 2]
GC = [(0, 20), (20, 22, 35)]
DLA = 4 + 1 + 2 * NT
VCR = 3


def build(nc, a, out, stop="D"):
    kh_d = nc.dram_tensor("k_hi", [NB * D, MP], F32).ap()
    kl_d = nc.dram_tensor("k_lo", [NB * D, MP], F32).ap()
    v_d = nc.dram_tensor("v_stack", [NJ, P, MT * VC], F32).ap()
    m_d = nc.dram_tensor("key_mask", [NJ, MP], F32).ap()

    with ExitStack() as ctx:
        def sbuf(stack, name, shape, dt=F32):
            return stack.enter_context(nc.sbuf_tensor(name, shape, dt))

        sb = lambda name, shape, dt=F32: sbuf(ctx, name, shape, dt)
        sem = lambda name: ctx.enter_context(nc.semaphore(name))

        resid = sb("resid", [P, NT, D])
        xn = sb("xn", [P, NT, D])
        xTh = sb("xTh", [P, KT, NT * P], F32R)
        xTl = sb("xTl", [P, KT, NT * P], F32R)
        st6 = sb("st6", [P, NT, 6])
        mv = sb("mv", [P, NT, 2])
        std = sb("std", [P, NT])
        rstd = sb("rstd", [P, NT])
        eps = sb("eps", [P, 1])
        ident = sb("ident", [P, P])
        zero = sb("zero", [P, 512], F32R)
        one_row = sb("one_row", [1, P], F32R)
        with ExitStack() as s:
            A = lambda name, shape, dt=F32: sbuf(s, name, shape, dt)
            raw = A("raw", [P, 2, 1024])
            cTh, cTl = A("cTh", [P, KT, MP], F32R), A("cTl", [P, KT, MP], F32R)
            cNh, cNl = A("cNh", [P, MT, D], F32R), A("cNl", [P, MT, D], F32R)
            wk_raw, wv_raw = A("wk_raw", [P, KT, D]), A("wv_raw", [P, KT, D])
            wkh, wkl = A("wkh", [P, KT, D], F32R), A("wkl", [P, KT, D], F32R)
            wvh, wvl = A("wvh", [P, KT, D], F32R), A("wvl", [P, KT, D], F32R)
            bk = A("bk", [P, KT])
            bv = A("bv", [P, D])
            xch, xcl = A("xch", [P, KT, SEQ], F32R), A("xcl", [P, KT, SEQ], F32R)
            attend_w = A("attend", [P, MW], I32)
            attend = attend_w[:].bitcast(U8)[:, 0:MP]
            neg = A("neg", [1, MP], F32R)
            valid = A("valid", [P, 1])
            mi = A("mi", [NPAIR, MP], I32)
            mneg = A("mneg", [NPAIR, MP])
            nmax = A("nmax", [P, 1])
            rmax = A("rmax", [P, 1])
            psum_ = A("psum_", [P, 1])
            rsum = A("rsum", [P, 1])
            rscale = A("rscale", [P, 1])
            prob = A("prob", [P, MP])
            pTh, pTl = A("pTh", [P, MT, P], F32R), A("pTl", [P, MT, P], F32R)
            k32 = A("k32", [P, 2, 512])
            kh, kl = A("kh", [P, 2, 512], F32R), A("kl", [P, 2, 512], F32R)
            v32 = A("v32", [P, 2, 2, D])
            vstk = A("vstk", [P, NPAIR, MT, VC], F32R)
        with ExitStack() as s:
            Bt = lambda name, shape, dt=F32: sbuf(s, name, shape, dt)
            w_raw = Bt("w_raw", [P, 2, WC])
            w_hi = Bt("w_hi", [P, 2, WC], F32R)
            w_lo = Bt("w_lo", [P, 2, 3 * D], F32R)
            silu = Bt("silu", [P, 2, 512])
            h32 = Bt("h32", [P, 2, 512])
            hh, hl = Bt("hh", [P, 2, 512], F32R), Bt("hl", [P, 2, 512], F32R)
            combh, combl = Bt("combh", [E, NT * P], F32R), Bt("combl", [E, NT * P], F32R)
            gw_raw = Bt("gw_raw", [P, KT, E])
            gwh, gwl = Bt("gwh", [P, KT, E], F32R), Bt("gwl", [P, KT, E], F32R)
            gb = Bt("gb", [P, E])
            tri16 = Bt("tri16", [P, E * E])
            tri4 = Bt("tri4", [P, 16])
            g_s = Bt("g_s", [P, NT, E])
            g_c = Bt("g_c", [P, NT, E])
            g_pair = Bt("g_pair", [P, NT * 4, 6])
            g_gs = Bt("g_gs", [P, NT * 4])
            g_gr = Bt("g_gr", [P, NT * 4])
            g_big = Bt("g_big", [P, NT * E, E])
            g_eq = Bt("g_eq", [P, NT * E, E])
            g_rank = Bt("g_rank", [P, NT, E])
            g_w = Bt("g_w", [P, NT, E])
            g_t = Bt("g_t", [P, NT])
            g_r = Bt("g_r", [P, NT])
        with ExitStack() as s:
            C = lambda name, shape, dt=F32: sbuf(s, name, shape, dt)
            qs = C("qs", [P, NJ, 2, SEQ], F32R)
            kslot = C("kslot", [P, 2, MP], F32R)
            vslot = C("vslot", [P, 2, MT * VC], F32R)
            p32 = C("p32", [P, 4, 1024])
            ph, pl = C("ph", [P, 2, 1024], F32R), C("pl", [P, 2, 1024], F32R)
            oT = C("oT", [VC, 2, 512])
            cx = C("cx", [P, 2, NJ, PR])
            wq_raw = C("wq_raw", [P, KT, NPAIR, 3 * PR])
            wqh, wql = C("wqh", [P, KT, NPAIR, 3 * PR], F32R), C("wql", [P, KT, NPAIR, 3 * PR], F32R)
            wo_raw = C("wo_raw", [P, KT, D])
            woh, wol = C("woh", [P, KT, D], F32R), C("wol", [P, KT, D], F32R)
            bq = C("bq", [P, NPAIR])
            hmask = C("hmask", [P, 2])
            bqm = C("bqm", [P, 2, NPAIR])
            bo = C("bo", [P, D])
            gam, bet = C("gam", [P, D]), C("bet", [P, D])
            rs = C("rs", [P, 1])
            q32 = C("q32", [P, 2, 512])
            msum = C("msum", [VC, 2, HD + 1])
            s4 = C("s4", [P, 2, 4])
            r4 = C("r4", [P, 2, 4])
        cTxh, cTxl = (t[:].rearrange("p k n -> p (k n)").rearrange("p (q n) -> p q n", n=512) for t in (xTh, xTl))
        dlt = xn

        ps = ctx.enter_context(nc.psum_tensor("ps", [P, 8, 512], F32))
        psf = ps[:, :, :].rearrange("p b n -> p (b n)")

        x_in, wkv_in, cst_in, gate_in, cw_in = sem("x_in"), sem("wkv_in"), sem("cst_in"), sem("gate_in"), sem("cw_in")
        cst_set = sem("cst_set")
        wkv_hi, wkv_rdy = sem("wkv_hi"), sem("wkv_rdy")
        ln_stat, ln_mv, ln_std, ln_rstd, ln_xn = (sem(n) for n in ("ln_stat", "ln_mv", "ln_std", "ln_rstd", "ln_xn"))
        ln_T, ln_hi, ln_lo = sem("ln_T"), sem("ln_hi"), sem("ln_lo")
        raw_in = [sem("raw_in0"), sem("raw_in1")]
        raw_free, split_hi = sem("raw_free"), sem("split_hi")
        ctxT_rdy, ctxN_rdy, ctxT_free, ctxN_free = sem("ctxT_rdy"), sem("ctxN_rdy"), sem("ctxT_free"), sem("ctxN_free")
        att_in, att_free, mi_in, mi_free = sem("att_in"), sem("att_free"), sem("mi_in"), sem("mi_free")
        mneg_a, mneg_rdy, md_out = sem("mneg_a"), sem("mneg_rdy"), sem("md_out")
        neg_rdy, xc_rdy, xc_free = sem("neg_rdy"), sem("xc_rdy"), sem("xc_free")
        S_rdy, max_rdy, nmax_rdy, exp_rdy = sem("S_rdy"), sem("max_rdy"), sem("nmax_rdy"), sem("exp_rdy")
        K_rdy, K_ev, k32_rdy, kl_rdy, k32_free = sem("K_rdy"), sem("K_ev"), sem("k32_rdy"), sem("kl_rdy"), sem("k32_free")
        k_out = [sem("k_out0"), sem("k_out1")]
        V_rdy, V_ev, vh_rdy, vl_rdy = sem("V_rdy"), sem("V_ev"), sem("vh_rdy"), sem("vl_rdy")
        v_out = sem("v_out")
        T_rdy, pTh_rdy, pTl_rdy = sem("T_rdy"), sem("pTh_rdy"), sem("pTl_rdy")
        R_rdy, R_ev, rs_chain = sem("R_rdy"), sem("R_ev"), sem("rs_chain")
        w_in = [sem("w_in0"), sem("w_in1")]
        w_hi_rdy, w_rdy, w_free = sem("w_hi_rdy"), sem("w_rdy"), sem("w_free")
        G_rdy, U_rdy, silu_rdy, mul1_rdy = sem("G_rdy"), sem("U_rdy"), sem("silu_rdy"), sem("mul1_rdy")
        C_rdy, mul2_rdy, hh_rdy, hl_rdy, down_done = sem("C_rdy"), sem("mul2_rdy"), sem("hh_rdy"), sem("hl_rdy"), sem("down_done")
        gwh_rdy, gw_rdy, L_rdy, g_act, g_chain = sem("gwh_rdy"), sem("gw_rdy"), sem("L_rdy"), sem("g_act"), sem("g_chain")
        gT_rdy, combh_rdy, combl_rdy = sem("gT_rdy"), sem("combh_rdy"), sem("combl_rdy")
        add_rdy = sem("add_rdy")
        cwh, cw_rdy, bq_rdy = sem("cwh"), sem("cw_rdy"), sem("bq_rdy")
        Q_rdy, q_hi, q_32, q_lo = sem("Q_rdy"), sem("q_hi"), sem("q_32"), sem("q_lo")
        kv_in = [sem("kv_in0"), sem("kv_in1")]
        k_free, v_free = sem("k_free"), sem("v_free")
        sc_rdy, p_exp, p_clip, ph_rdy, pl_rdy, pv_done = (sem(n) for n in ("sc_rdy", "p_exp", "p_clip", "ph_rdy", "pl_rdy", "pv_done"))
        o_rdy, oT_rdy, osum_rdy, s4_rdy, r4_rdy, cx_rdy = (sem(n) for n in ("o_rdy", "oT_rdy", "osum_rdy", "s4_rdy", "r4_rdy", "cx_rdy"))
        cT_rdy, cTh_rdy, cTl_rdy, dl_rdy, dl_a, dl_std, dl_b = (sem(n) for n in ("cT_rdy", "cTh_rdy", "cTl_rdy", "dl_rdy", "dl_a", "dl_std", "dl_b"))
        pool_go = sem("pool_go")
        out_done, out_go = sem("out_done"), sem("out_go")
        valid_rdy, rsum_rdy, rscale_rdy = sem("valid_rdy"), sem("rsum_rdy"), sem("rscale_rdy")
        q_set, pl_free, wraw_free = sem("q_set"), sem("pl_free"), sem("wraw_free")

        block = ctx.enter_context(nc.Block())

        FFN = {"B": dict(w=a["w0"], sh=NSH0, ex=NEX0, t0=0, n=0, ln=1, gw=a["gw0"], gb=a["gb0"]),
               "D": dict(w=a["w1"], sh=NSH1, ex=NEX1, t0=NSH0 + NEX0, n=1, ln=3, gw=a["gw1"], gb=a["gb1"])}
        for f in FFN.values():
            f["c0"] = 2 * f["t0"]
            f["e0"] = 2 * NEX0 * f["n"]
            f["p0"] = f["c0"]

        def store(sp):
            sp.wait_ge(out_go, 1)
            sp.dma_start(out.rearrange("(t p) d -> p t d", p=P), resid[:]).then_inc(out_done, 16)
            sp.wait_ge(out_done, 16)

        @block.sync
        def _(sp):
            sp.dma_start(resid[:], a["x"].rearrange("(t p) d -> p t d", p=P)).then_inc(x_in, 16)
            for t, s in ((wk_raw, a["wkT"]), (wv_raw, a["wvT"])):
                sp.dma_start(t[:], s.rearrange("(k p) n -> p k n", p=P)).then_inc(wkv_in, 16)
            sp.dma_start(bk[:], a["bk"]).then_inc(wkv_in, 16)
            sp.dma_start(bv[:], a["bv"].rearrange("(o n) -> o n", o=1).broadcast_to([P, D])).then_inc(wkv_in, 16)
            sp.dma_start(ident[:], a["ident"]).then_inc(cst_in, 16)

            with sp.Fori(0, NB) as b:
                sp.wait_ge(att_free, b + 1)
                sp.dma_start(attend_w[:], a["attend"][bass.ds(b, 1), :].broadcast_to([P, MW])).then_inc(att_in, 16)
                sp.wait_ge(mi_free, b + 1)
                sp.dma_start(mi[:], a["keep"][bass.ds(b, 1), :].broadcast_to([NPAIR, MP])).then_inc(mi_in, 16)
                for n, (kind, k, c0, w) in enumerate(PIECES):
                    sp.wait_ge(raw_free, b * NP_ + (n + 1))
                    if kind == "t":
                        src = a["ctxT"][bass.ds(b * KT + k, 1), :, c0:c0 + w].rearrange("o p n -> (o p) n")
                        dst = raw[:, n % 2, 0:w]
                    else:
                        src = a["ctxN"][bass.ds(b, 1), c0 * P:(c0 + w) * P, :].rearrange("o (t p) d -> p (o t) d", p=P)
                        dst = raw[:, n % 2, 0:w * D].rearrange("p (t d) -> p t d", d=D)
                    sp.dma_start(dst, src).then_inc(raw_in[n % 2], 16)
                sp.wait_ge(mneg_rdy, b + 1)
                sp.dma_start(m_d[bass.ds(b * NPAIR, NPAIR), :], mneg[:]).then_inc(md_out, 16)
                for n in range(8):
                    mt, (c0, w) = n // 4, MCH[n % 4]
                    sp.wait_ge(kl_rdy, b * 8 + (n + 1))
                    for t, dr in ((kh, kh_d), (kl, kl_d)):
                        sp.dma_start(dr[bass.ds(b * D + mt * P, P), c0:c0 + w], t[:, n % 2, 0:w].bitcast(F32)).then_inc(k_out[n % 2], 16)
                sp.wait_ge(vl_rdy, b * 8 + 8)
                sp.dma_start(v_d[bass.ds(b * NPAIR, NPAIR), :, :].rearrange("t p n -> p t n"),
                             vstk[:].bitcast(F32).rearrange("p t m c -> p t (m c)")).then_inc(v_out, 16)

            def load_ffn(f):
                for t, s in ((tri16, a["tri16"]), (tri4, a["tri4"]), (gb, f["gb"].rearrange("(o n) -> o n", o=1).broadcast_to([P, E])),
                             (gw_raw, f["gw"].rearrange("(k p) n -> p k n", p=P))):
                    sp.dma_start(t[:], s).then_inc(gate_in, 16)
                for k in range(f["sh"]):
                    tile(f, 0, k)
                with sp.Fori(0, f["ex"] // 2) as i:
                    for j in range(2):
                        tile(f, i * 2, f["sh"] + j)

            def tile(f, i, k):
                slot = (f["t0"] + k) % 2
                sp.wait_ge(wraw_free, i + (f["t0"] + k + 1))
                sp.dma_start(w_raw[:, slot, :], f["w"][bass.ds(i + k, 1)].rearrange("o p n -> (o p) n")).then_inc(w_in[slot], 16)

            if stop == "A":
                return store(sp)
            sp.wait_ge(ln_stat, 2)
            for n in range(2):
                sp.wait_ge(k_out[n], 32 * (NB * 4 + 1))
            sp.wait_ge(v_out, 16 * (NB + 1))
            sp.wait_ge(md_out, 16 * (NB + 1))
            load_ffn(FFN["B"])
            if stop == "B":
                return store(sp)

            sp.wait_ge(ln_stat, 3)
            for r in range(3):
                for k in range(KT):
                    sp.dma_start(wq_raw[:, k, :, PR * r:PR * r + PR], a["wqT"][k * P:(k + 1) * P, :].rearrange("p (t n) -> p t n", n=PR)).then_inc(cw_in, 16)
                sp.dma_start(bq[PR * r:PR * r + PR, :], a["bq"]).then_inc(cw_in, 16)
            for t, s in ((wo_raw[:], a["woT"].rearrange("(k p) n -> p k n", p=P)), (hmask[:], a["hmask"]), (msum[:], a["msum"]),
                         (bo[:], a["bo"].rearrange("(o n) -> o n", o=1).broadcast_to([P, D])),
                         (gam[:], a["gam"].rearrange("(o n) -> o n", o=1).broadcast_to([P, D])),
                         (bet[:], a["bet"].rearrange("(o n) -> o n", o=1).broadcast_to([P, D])),
                         (rs[:], a["rs"].rearrange("(o n) -> o n", o=1).broadcast_to([P, 1]))):
                sp.dma_start(t, s).then_inc(cw_in, 16)
            with sp.Fori(0, NJ // 2) as i:
                for u in range(2):
                    sp.wait_ge(k_free, i * 2 + (u + 1))
                    sp.wait_ge(v_free, i * 2 + (u + 1))
                    rows = bass.ds(i * (2 * PR) + u * PR, PR)
                    for r, dr in enumerate((kh_d, kl_d, kh_d)):
                        sp.dma_start(kslot[PR * r:PR * r + PR, u, :].bitcast(F32), dr[rows, :]).then_inc(kv_in[u], 16)
                    job = bass.ds(i * 2 + u, 1)
                    sp.dma_start(kslot[3 * PR:QROWS, u, :].bitcast(F32), m_d[job, :]).then_inc(kv_in[u], 16)
                    sp.dma_start(vslot[:, u, :].bitcast(F32), v_d[job].rearrange("o p n -> (o p) n")).then_inc(kv_in[u], 16)
            if stop == "C":
                return store(sp)
            sp.wait_ge(ln_stat, 4)
            load_ffn(FFN["D"])
            store(sp)

        @block.gpsimd
        def _(pool):
            pool.memset(zero[:].bitcast(F32), 0.0).then_inc(cst_set, 1)
            pool.memset(one_row[:].bitcast(F32), 1.0).then_inc(cst_set, 1)
            pool.memset(eps[:], EPS).then_inc(cst_set, 1)
            pool.memset(vstk[:].bitcast(F32), 0.0).then_inc(cst_set, 1)
            pool.wait_ge(cst_set, 4)
            pool.memset(vstk[:, :, :, 2 * PR:VC].bitcast(F32), 1.0).then_inc(cst_set, 1)
            pool.sem_inc(raw_free, 2)
            pool.sem_inc(mi_free, 1)
            pool.sem_inc(md_out, 16)
            with pool.Fori(0, NB) as b:
                for n, (kind, k, c0, w) in enumerate(PIECES):
                    if n == 0:
                        pool.wait_ge(ctxT_free, b + 1)
                    if n == 4:
                        pool.wait_ge(ctxN_free, b + 1)
                    pool.wait_ge(raw_in[n % 2], b * (16 * NP_ // 2) + 16 * (n // 2 + 1))
                    if kind == "t":
                        hi, lo, src = cTh[:, k, c0:c0 + w], cTl[:, k, c0:c0 + w], raw[:, n % 2, 0:w]
                    else:
                        hi, lo = cNh[:, c0:c0 + w, :], cNl[:, c0:c0 + w, :]
                        src = raw[:, n % 2, 0:w * D].rearrange("p (t d) -> p t d", d=D)
                    pool.sem_inc(pool_go, 1)
                    pool.tensor_copy(hi, src).then_inc(split_hi, 1)
                    pool.wait_ge(split_hi, b * NP_ + (n + 1))
                    pool.tensor_tensor(lo, src, hi.bitcast(F32), ALU.subtract).then_inc(ctxT_rdy if kind == "t" else ctxN_rdy, 1)
                    pool.wait_ge(ctxT_rdy if kind == "t" else ctxN_rdy, b * 4 + (n % 4 + 1))
                    pool.sem_inc(raw_free, 1)
                pool.wait_ge(mi_in, b * 16 + 16)
                pool.wait_ge(md_out, b * 16 + 16)
                pool.sem_inc(pool_go, 1)
                pool.tensor_scalar(mneg[:], mi[:], 0.5, 1.0, ALU.is_gt, ALU.subtract).then_inc(mneg_a, 1)
                pool.wait_ge(mneg_a, b + 1)
                pool.sem_inc(pool_go, 1)
                pool.tensor_scalar(mneg[:], mneg[:], 4e30, None, ALU.mult).then_inc(mneg_rdy, 1)
                pool.wait_ge(mneg_rdy, b + 1)
                pool.sem_inc(mi_free, 1)

        def mm3(e, o, lh, ll, rh, rl, first, last):
            e.matmul(o, lh, rh, start=first, stop=False, skip_group_check=True)
            e.matmul(o, lh, rl, start=False, stop=False, skip_group_check=True)
            return e.matmul(o, ll, rh, start=False, stop=last, skip_group_check=True)

        @block.tensor
        def _(pe):
            def ln_transpose(n):
                for q in range(4):
                    pe.wait_ge(ln_xn, 8 * n + 2 * q + 2)
                    for k in range(KT):
                        for j in range(2):
                            mm = pe.transpose(ps[:, q, (2 * k + j) * P:(2 * k + j + 1) * P], xn[:, 2 * q + j, k * P:(k + 1) * P], ident[:])
                    mm.then_inc(ln_T, 1)

            pe.wait_ge(cst_in, 16)
            pe.wait_ge(cst_set, 5)
            ln_transpose(0)
            pe.sem_inc(ctxT_free, 1)
            pe.sem_inc(ctxN_free, 1)
            pe.sem_inc(xc_free, 1)
            pe.sem_inc(R_rdy, 1)
            pe.wait_ge(wkv_rdy, 4)
            pe.wait_ge(ln_lo, 4)

            with pe.Fori(0, NB) as b:
                for st in range(2):
                    def kproj(n):
                        mt, (c0, w) = n // 4, MCH[n % 4]
                        o = ps[:, 6 + n % 2, 0:w]
                        if n % 4 < 2:
                            pe.wait_ge(V_ev, b * 8 + (4 * (n // 4) + n % 2 - 2 + 1 + VCR))
                        else:
                            pe.wait_ge(K_ev, b * 8 + (n - 2 + 1))
                        for k in range(KT):
                            mm = mm3(pe, o, wkh[:, k, mt * P:(mt + 1) * P], wkl[:, k, mt * P:(mt + 1) * P],
                                     cTh[:, k, c0:c0 + w], cTl[:, k, c0:c0 + w], k == 0, k == KT - 1)
                        mm.then_inc(K_rdy, 1)

                    def vproj(n):
                        m0, cnt = VUNITS[n]
                        if n % 4 < 2:
                            pe.wait_ge(K_ev, b * 8 + (4 * (n // 4) + 2 + n % 2 + 1))
                        else:
                            pe.wait_ge(V_ev, b * 8 + (n - 2 + 1 + VCR))
                        for i in range(cnt):
                            rows = TAIL if m0 + i == MT - 1 else P
                            for k in range(KT):
                                s = slice((m0 + i) * P, (m0 + i) * P + rows)
                                mm = mm3(pe, ps[0:rows, 6 + n % 2, i * D:(i + 1) * D], cTh[:, k, s], cTl[:, k, s],
                                         wvh[:, k, :], wvl[:, k, :], k == 0, k == KT - 1)
                        mm.then_inc(V_rdy, 1)
                        return mm

                    def trans(g):
                        if g >= 2:
                            pe.wait_ge(pTl_rdy, b * 8 + (4 * st + g - 2 + 1))
                        for m in range(4 * g, min(4 * g + 4, MT)):
                            rows = TAIL if m == MT - 1 else P
                            mm = pe.transpose(ps[0:rows, 4 + g % 2, (m % 4) * P:(m % 4 + 1) * P], prob[:, m * P:m * P + rows], ident[:])
                        mm.then_inc(T_rdy, 1)

                    if st == 0:
                        pe.wait_ge(xc_rdy, b + 1)
                        pe.wait_ge(neg_rdy, b + 1)
                        pe.wait_ge(ctxT_rdy, b * 4 + 4)
                    for c in (1, 2, 3, 0):
                        c0, w = MCH[c]
                        if c == 0:
                            pe.wait_ge(R_ev, b * 2 + (st + 1))
                        for k in range(KT):
                            mm3(pe, ps[:, c, 0:w], xch[:, k, st * P:(st + 1) * P], xcl[:, k, st * P:(st + 1) * P],
                                cTh[:, k, c0:c0 + w], cTl[:, k, c0:c0 + w], k == 0, False)
                        mm = pe.matmul(ps[:, c, 0:w], one_row[:], neg[:, c0:c0 + w], start=False, stop=True, skip_group_check=True)
                    mm.then_inc(S_rdy, 1)
                    kproj(4 * st)
                    kproj(4 * st + 1)
                    pe.wait_ge(exp_rdy, b * 2 + (st + 1))
                    trans(0)
                    trans(1)
                    kproj(4 * st + 2)
                    kproj(4 * st + 3)
                    trans(2)
                    trans(3)
                    for n in range(4 * st, 4 * st + 4):
                        vproj(n)
                    pe.wait_ge(pTl_rdy, b * 8 + (4 * st + 4))
                    if st == 0:
                        pe.wait_ge(ctxN_rdy, b * 4 + 4)
                    for m in range(MT):
                        rows = TAIL if m == MT - 1 else P
                        mm = mm3(pe, ps[:, 0, 0:D], pTh[0:rows, m, :], pTl[0:rows, m, :], cNh[0:rows, m, :], cNl[0:rows, m, :], m == 0, m == MT - 1)
                    mm.then_inc(R_rdy, 1)
                pe.wait_ge(R_rdy, b * 2 + 3)
                pe.sem_inc(ctxT_free, 1)
                pe.sem_inc(ctxN_free, 1)
                pe.sem_inc(xc_free, 1)
            if stop == "A":
                return

            def ffn(f):
                sh, ex, c0, e0, n = f["sh"], f["ex"], f["c0"], f["e0"], f["n"]
                ln_transpose(f["ln"])
                pe.wait_ge(ln_lo, 4 * f["ln"] + 4)
                pe.wait_ge(gw_rdy, n + 1)
                for t in range(NT):
                    for k in range(KT):
                        s = slice(t * P, (t + 1) * P)
                        mm = mm3(pe, ps[:, 4, t * E:(t + 1) * E], xTh[:, k, s], xTl[:, k, s], gwh[:, k, :], gwl[:, k, :], k == 0, k == KT - 1)
                mm.then_inc(L_rdy, 1)
                pe.wait_ge(g_chain, GC[n][-1])
                for t in range(NT):
                    mm = pe.transpose(ps[0:E, 5 + t // 4, (t % 4) * P:(t % 4 + 1) * P], g_w[:, t, :], ident[:])
                mm.then_inc(gT_rdy, 1)
                for q in range(4):
                    mm = pe.matmul(ps[:, q, :], zero[:, 0:P], zero[:], start=True, stop=False, skip_group_check=True)
                pe.wait_ge(combl_rdy, n + 1)

                def hidden(ct, slot, half, exp, first, ec):
                    s = slice(half * 512, half * 512 + 512)
                    if half == 0:
                        pe.wait_ge(w_rdy, tile_no(ct))
                    if not first:
                        pe.wait_ge(silu_rdy, ct)
                    for k in range(KT):
                        mm = mm3(pe, ps[:, 4, :], w_hi[:, slot, k * P:(k + 1) * P], w_lo[:, slot, k * P:(k + 1) * P], xTh[:, k, s], xTl[:, k, s], k == 0, k == 1)
                    mm.then_inc(G_rdy, 1)
                    if not first:
                        pe.wait_ge(mul1_rdy, ct)
                    for k in range(KT):
                        w = slice(D + k * P, D + (k + 1) * P)
                        mm = mm3(pe, ps[:, 5, :], w_hi[:, slot, w], w_lo[:, slot, w], xTh[:, k, s], xTl[:, k, s], k == 0, k == 1)
                    mm.then_inc(U_rdy, 1)
                    if exp:
                        if ec is not None:
                            pe.wait_ge(mul2_rdy, ec)
                        sel = w_hi[0:E, slot, 3 * D:WC]
                        pe.matmul(ps[:, 6, :], sel, combh[:, s], start=True, stop=False, skip_group_check=True)
                        pe.matmul(ps[:, 6, :], sel, combl[:, s], start=False, stop=True, skip_group_check=True).then_inc(C_rdy, 1)

                def down(ct, slot, half):
                    pe.wait_ge(hl_rdy, ct + 1)
                    buf = half
                    for j in range(4):
                        t = 4 * half + j
                        s = slice(j * P, (j + 1) * P)
                        mm = mm3(pe, ps[:, t // 2, (t % 2) * D:(t % 2 + 1) * D], hh[:, buf, s], hl[:, buf, s],
                                 w_hi[:, slot, 2 * D:3 * D], w_lo[:, slot, 2 * D:3 * D], False, False)
                    mm.then_inc(down_done, 1)
                    if half == 1:
                        mm_free(ct)

                def tile_no(ct):
                    return ct_tiles[0]

                ct_tiles = [None]

                def mm_free(ct):
                    pe.wait_ge(down_done, ct + 1)
                    pe.sem_inc(w_free, 1)

                prev = None
                for k in range(sh):
                    for half in range(2):
                        ct = c0 + 2 * k + half
                        ct_tiles[0] = f["t0"] + k + 1
                        slot = (f["t0"] + k) % 2
                        hidden(ct, slot, half, False, k == 0 and half == 0 and n == 0, None)
                        if prev:
                            down(*prev)
                        prev = (ct, slot, half)
                tb = f["t0"] + sh

                def step(i, j, half, first):
                    ct = i * 4 + (2 * tb + 2 * j + half)
                    slot = (tb + j) % 2
                    ct_tiles[0] = i * 2 + (tb + j + 1)
                    ec = None if (first and n == 0) else i * 4 + (e0 + 2 * j + half)
                    hidden(ct, slot, half, True, False, ec)
                    pct = i * 4 + (2 * tb + 2 * j + half - 1)
                    down(pct, slot if half else (tb + j - 1) % 2, (half + 1) % 2)

                for j in range(2):
                    for half in range(2):
                        step(0, j, half, j == 0 and half == 0)
                with pe.Fori(1, ex // 2) as i:
                    for j in range(2):
                        for half in range(2):
                            step(i, j, half, False)
                last = 2 * (tb + ex) - 1
                down(last, (tb + ex - 1) % 2, 1)

            pe.sem_inc(w_free, 2)
            ffn(FFN["B"])
            if stop == "B":
                return

            ln_transpose(2)
            pe.wait_ge(ln_lo, 12)
            pe.wait_ge(cw_rdy, 4)
            for n in range(2 * NPAIR):
                t, half = n // 2, n % 2
                s = slice(half * 512, half * 512 + 512)
                if n >= 4:
                    pe.wait_ge(q_32, 2 * (n - 4) + 2)
                    pe.wait_ge(q_hi, 2 * (n - 4) + 2)
                for k in range(KT):
                    mm = mm3(pe, ps[0:3 * PR, 4 + n % 4, :], wqh[:, k, t, :], wql[:, k, t, :], xTh[:, k, s], xTl[:, k, s], k == 0, k == 1)
                mm.then_inc(Q_rdy, 1)
            pe.wait_ge(q_lo, 4 * NPAIR)
            pe.wait_ge(q_set, 1)

            pe.sem_inc(k_free, 2)
            pe.sem_inc(v_free, 2)

            def qk(i, u, c):
                g = i * (2 * NCH) + (u * NCH + c)
                if c == 0:
                    pe.wait_ge(kv_in[u], i * 80 + 80)
                bank = 2 * ((u * NCH + c) % 2)
                pe.wait_ge(p_exp, g + 1)
                for m in range(2 * c, min(2 * c + 2, MT)):
                    rows = TAIL if m == MT - 1 else P
                    mm = pe.matmul(ps[0:rows, bank + m % 2, :], kslot[0:QROWS, u, m * P:m * P + rows],
                                   qs[0:QROWS, bass.ds(i * 2 + u, 1), :, :].rearrange("p o h s -> p (o h s)"), start=True, stop=True)
                mm.then_inc(sc_rdy, 1)

            def pv(i, u, c):
                g = i * (2 * NCH) + (u * NCH + c)
                if c == 0:
                    pe.wait_ge(oT_rdy, i * 2 + (u + 1))
                pe.wait_ge(pl_rdy, g + 1)
                buf = (u * NCH + c) % 2
                for m in range(2 * c, min(2 * c + 2, MT)):
                    rows = TAIL if m == MT - 1 else P
                    v = vslot[0:rows, u, m * VC:(m + 1) * VC]
                    s = slice((m % 2) * 512, (m % 2) * 512 + 512)
                    pe.matmul(ps[0:VC, 4 + u, :], v, ph[0:rows, buf, s], start=(m == 0), stop=False, skip_group_check=True)
                    mm = pe.matmul(ps[0:VC, 4 + u, :], v, pl[0:rows, buf, s], start=False, stop=(m == MT - 1), skip_group_check=True)
                mm.then_inc(pv_done, 1)
                if c == NCH - 1:
                    pe.wait_ge(pv_done, g + 2 + 1)
                    pe.sem_inc(v_free, 1)
                    pe.sem_inc(o_rdy, 1)

            def osum(i, u):
                pe.wait_ge(oT_rdy, i * 2 + (u + 1 + 2))
                pe.wait_ge(cx_rdy, i * 2 + (u + 1))
                for h in range(2):
                    for st in range(2):
                        mm = pe.matmul(ps[:, 6, (2 * h + st) * 32:(2 * h + st) * 32 + HD + 1],
                                       oT[:, u, h * SEQ + st * P:h * SEQ + (st + 1) * P], msum[:, h, :], start=True, stop=True)
                mm.then_inc(osum_rdy, 1)

            def job_pair(i, first, last):
                for x in range(2 * NCH):
                    y = x + 2
                    if y < 2 * NCH:
                        qk(i, y // NCH, y % NCH)
                        if y % NCH == NCH - 1:
                            pe.wait_ge(sc_rdy, i * (2 * NCH) + (y + 1))
                            pe.sem_inc(k_free, 1)
                    elif not last:
                        qk(i + 1, 0, y - 2 * NCH)
                    if x == 3 and not first:
                        osum(i - 1, 1)
                    if x == NCH + 3:
                        osum(i, 0)
                    pv(i, x // NCH, x % NCH)

            pe.sem_inc(pv_done, 2)
            qk(0, 0, 0)
            qk(0, 0, 1)
            job_pair(0, True, False)
            with pe.Fori(1, NJ // 2 - 1) as i:
                job_pair(i, False, False)
            job_pair(NJ // 2 - 1, False, True)
            osum(NJ // 2 - 1, 1)

            pe.wait_ge(cx_rdy, NJ + 1)
            for q in range(4):
                for k in range(KT):
                    for j in range(2):
                        src = cx[:, j, q * NPAIR + 4 * k:q * NPAIR + 4 * k + 4, :].rearrange("p t r -> p (t r)")
                        mm = pe.transpose(ps[:, q, (2 * k + j) * P:(2 * k + j + 1) * P], src, ident[:])
                mm.then_inc(cT_rdy, 1)
            for q in range(4):
                pe.wait_ge(cTl_rdy, q + 1)
                for j in range(2):
                    for k in range(KT):
                        s = slice((2 * k + j) * P, (2 * k + j + 1) * P)
                        mm = mm3(pe, ps[:, 4 + q, j * D:(j + 1) * D], cTxh[:, q, s], cTxl[:, q, s], woh[:, k, :], wol[:, k, :], k == 0, k == 1)
                mm.then_inc(dl_rdy, 1)
            if stop == "C":
                return
            ffn(FFN["D"])

        @block.scalar
        def _(act):
            def ln_std_hi(n):
                act.wait_ge(ln_mv, 8 * n + 8)
                act.activation(std[:], mv[:, :, 1], ACT.Sqrt, bias=eps[:]).then_inc(ln_std, 1)
                for q in range(4):
                    act.wait_ge(ln_T, 4 * n + q + 1)
                    act.activation(xTh[:, :, q * 256:(q + 1) * 256], ps[:, q, :].rearrange("p (k n) -> p k n", k=KT), ACT.Copy).then_inc(ln_hi, 1)

            act.wait_ge(cst_set, 5)
            ln_std_hi(0)
            act.sem_inc(v_out, 16)
            for n in range(2):
                act.sem_inc(k_out[n], 32)
            with act.Fori(0, NB) as b:
                for st in range(2):
                    def kev(n):
                        mt, (c0, w) = n // 4, MCH[n % 4]
                        act.wait_ge(K_rdy, b * 8 + (n + 1))
                        act.wait_ge(k32_free, b * 8 + (n + 1))
                        act.wait_ge(k_out[n % 2], b * 128 + (32 * (n // 2) + 32))
                        act.activation(k32[:, n % 2, 0:w], ps[:, 6 + n % 2, 0:w], ACT.Identity, bias=bk[:, mt:mt + 1]).then_inc(k32_rdy, 1)
                        act.activation(kh[:, n % 2, 0:w], ps[:, 6 + n % 2, 0:w], ACT.Identity, bias=bk[:, mt:mt + 1]).then_inc(K_ev, 1)

                    def pth(g):
                        act.wait_ge(T_rdy, b * 8 + (4 * st + g + 1))
                        if g < 3:
                            act.activation(pTh[:, 4 * g:4 * g + 4, :], ps[:, 4 + g % 2, :].rearrange("p (m s) -> p m s", s=P), ACT.Copy).then_inc(pTh_rdy, 1)
                        else:
                            act.activation(pTh[0:TAIL, MT - 1, :], ps[0:TAIL, 5, 0:P], ACT.Copy).then_inc(pTh_rdy, 1)

                    kev(4 * st)
                    act.wait_ge(nmax_rdy, b * 2 + (st + 1))
                    act.activation(prob[:, 0:MP], psf[:, 0:MP], ACT.Exp, scale=1.0 / 16, bias=nmax[:], accum_out=psum_[:]).then_inc(exp_rdy, 1)
                    kev(4 * st + 1)
                    act.wait_ge(R_rdy, b * 2 + (st + 1))
                    pth(0)
                    pth(1)
                    kev(4 * st + 2)
                    kev(4 * st + 3)
                    pth(2)
                    pth(3)
                    for n in range(4 * st, 4 * st + 4):
                        m0, cnt = VUNITS[n]
                        rows = TAIL if m0 == MT - 1 else P
                        if n == 0:
                            act.wait_ge(v_out, b * 16 + 16)
                        act.wait_ge(V_ev, b * 8 + (n + 1 + VCR))
                        for i in range(cnt):
                            h = act.activation(vstk[0:rows, :, m0 + i, 0:PR], v32[0:rows, n % 2, i, :].rearrange("p (t r) -> p t r", r=PR), ACT.Copy)
                        h.then_inc(vh_rdy, 1)
            if stop == "A":
                return

            def ffn(f):
                n, c0, sh, ex = f["n"], f["c0"], f["sh"], f["ex"]
                ln_std_hi(f["ln"])
                act.wait_ge(L_rdy, n + 1)
                lg = ps[:, 4, 0:NT * E]
                if n == 0:
                    act.activation(g_s[:].rearrange("p t e -> p (t e)"), lg, ACT.Sigmoid).then_inc(g_act, 1)
                else:
                    act.wait_ge(g_chain, GC[1][1])
                    act.activation(g_s[:].rearrange("p t e -> p (t e)"), g_c[:].rearrange("p t e -> p (t e)"), ACT.Exp).then_inc(g_act, 1)
                act.wait_ge(gT_rdy, n + 1)
                act.activation(combh[:].rearrange("e (b s) -> e b s", b=2), ps[0:E, 5:7, :], ACT.Copy).then_inc(combh_rdy, 1)

                def chunk(ct, half, mulsem, mulval, wait_hh=True):
                    act.wait_ge(G_rdy, ct + 1)
                    act.activation(silu[:, half, :], ps[:, 4, :], ACT.Silu).then_inc(silu_rdy, 1)
                    act.wait_ge(mulsem, mulval)
                    if wait_hh:
                        act.wait_ge(down_done, ct - 1)
                    act.activation(hh[:, half, :], h32[:, half, :], ACT.Copy).then_inc(hh_rdy, 1)

                for k in range(sh):
                    for half in range(2):
                        ct = c0 + 2 * k + half
                        chunk(ct, half, mul1_rdy, ct + 1, ct >= 2)
                with act.Fori(0, ex // 2) as i:
                    for j in range(4):
                        ct = i * 4 + (c0 + 2 * sh + j)
                        chunk(ct, j % 2, mul2_rdy, i * 4 + (f["e0"] + j + 1))

            ffn(FFN["B"])
            if stop == "B":
                return

            ln_std_hi(2)
            act.wait_ge(bq_rdy, 1)
            for n in range(2 * NPAIR):
                t, half = n // 2, n % 2
                act.wait_ge(Q_rdy, n + 1)
                for h in range(2):
                    if 2 * n + h >= 2:
                        act.wait_ge(q_lo, 2 * n + h - 1)
                    act.activation(q32[2 * PR:3 * PR, h, :], ps[2 * PR:3 * PR, 4 + n % 4, :], ACT.Identity,
                                   scale=hmask[2 * PR:3 * PR, h:h + 1], bias=bqm[2 * PR:3 * PR, h, t:t + 1]).then_inc(q_32, 1)
            act.sem_inc(p_exp, 2)
            act.sem_inc(oT_rdy, 2)

            def exp_chunk(i, u, c):
                g = i * (2 * NCH) + (u * NCH + c)
                bank = 2 * ((u * NCH + c) % 2)
                act.wait_ge(sc_rdy, g + 1)
                act.wait_ge(pl_free, g + 1)
                rows, w = (P, 1024) if c < NCH - 1 else (TAIL, 512)
                act.activation(p32[0:rows, PSLOT[c], 0:w], psf[0:rows, bank * 512:bank * 512 + w], ACT.Exp, scale=0.25).then_inc(p_exp, 1)

            def hi_chunk(i, u, c):
                g = i * (2 * NCH) + (u * NCH + c)
                act.wait_ge(p_clip, g + 1)
                act.wait_ge(pv_done, g + 1)
                rows, w = (P, 1024) if c < NCH - 1 else (TAIL, 512)
                act.activation(ph[0:rows, (u * NCH + c) % 2, 0:w], p32[0:rows, PSLOT[c], 0:w], ACT.Copy).then_inc(ph_rdy, 1)

            def evac(i, u):
                act.wait_ge(o_rdy, i * 2 + (u + 1))
                act.activation(oT[:, u, :], ps[0:VC, 4 + u, :], ACT.Copy).then_inc(oT_rdy, 1)

            def job_pair(i, first, last):
                for x in range(2 * NCH):
                    y = x + 1
                    if y < 2 * NCH:
                        exp_chunk(i, y // NCH, y % NCH)
                    elif not last:
                        exp_chunk(i + 1, 0, 0)
                    if x == 2 and not first:
                        evac(i - 1, 1)
                    if x == NCH + 2:
                        evac(i, 0)
                    hi_chunk(i, x // NCH, x % NCH)

            exp_chunk(0, 0, 0)
            job_pair(0, True, False)
            with act.Fori(1, NJ // 2 - 1) as i:
                job_pair(i, False, False)
            job_pair(NJ // 2 - 1, False, True)
            evac(NJ // 2 - 1, 1)
            for q in range(4):
                act.wait_ge(cT_rdy, q + 1)
                act.activation(cTxh[:, q, :], ps[:, q, :], ACT.Copy).then_inc(cTh_rdy, 1)
            act.wait_ge(dl_a, DLA)
            act.activation(std[:], mv[:, :, 1], ACT.Sqrt, bias=eps[:]).then_inc(dl_std, 1)
            if stop == "C":
                return
            ffn(FFN["D"])

        @block.vector
        def _(dve):
            def ln_front(n):
                for t in range(NT):
                    s = dve.bn_stats(st6[:, t, :], resid[:, t, :])
                s.then_inc(ln_stat, 1)
                dve.wait_ge(ln_stat, n + 1)
                for t in range(NT):
                    dve.bn_aggr(mv[:, t, :], st6[:, t, :]).then_inc(ln_mv, 1)
                dve.wait_ge(ln_std, n + 1)
                dve.reciprocal(rstd[:], std[:]).then_inc(ln_rstd, 1)
                dve.wait_ge(ln_rstd, n + 1)
                for t in range(NT):
                    dve.tensor_scalar(xn[:, t, :], resid[:, t, :], mv[:, t, 0:1], rstd[:, t:t + 1], ALU.subtract, ALU.mult).then_inc(ln_xn, 1)

            def ln_back(n):
                for q in range(4):
                    dve.wait_ge(ln_hi, 4 * n + q + 1)
                    s = slice(q * 256, (q + 1) * 256)
                    dve.tensor_tensor(xTl[:, :, s], ps[:, q, :].rearrange("p (k n) -> p k n", k=KT), xTh[:, :, s].bitcast(F32), ALU.subtract).then_inc(ln_lo, 1)

            def rank(link, v, out_, tri, w):
                a_, b_ = (g_big, g_eq)
                eq = b_[:].rearrange("p a b -> p (a b)")[:, 0:NT * w * w]
                big = a_[:].rearrange("p a b -> p (a b)")[:, 0:NT * w * w]
                b4 = big.rearrange("p (t e j) -> p t e j", e=w, j=w)
                e4 = eq.rearrange("p (t e j) -> p t e j", e=w, j=w)
                vj = v.unsqueeze(2).broadcast_to([P, NT, w, w])
                ve = v.unsqueeze(3).broadcast_to([P, NT, w, w])
                dve.tensor_tensor(b4, vj, ve, ALU.is_gt)
                link(dve.tensor_tensor(e4, vj, ve, ALU.is_equal))
                tb_ = tri[:].unsqueeze(1).broadcast_to([P, NT, w * w])
                link(dve.tensor_tensor(eq.rearrange("p (t n) -> p t n", n=w * w), eq.rearrange("p (t n) -> p t n", n=w * w), tb_, ALU.mult))
                link(dve.tensor_tensor(big, big, eq, ALU.add))
                link(dve.tensor_reduce(out_, big.rearrange("p (a j) -> p a j", j=w), AX.X, ALU.add))

            dve.wait_ge(x_in, 16)
            ln_front(0)
            dve.wait_ge(wkv_in, 64)
            for r, h, l in ((wk_raw, wkh, wkl), (wv_raw, wvh, wvl)):
                dve.tensor_copy(h[:], r[:]).then_inc(wkv_hi, 1)
            dve.wait_ge(wkv_hi, 2)
            for r, h, l in ((wk_raw, wkh, wkl), (wv_raw, wvh, wvl)):
                dve.tensor_tensor(l[:], r[:], h[:].bitcast(F32), ALU.subtract).then_inc(wkv_rdy, 2)
            ln_back(0)
            dve.sem_inc(att_free, 1)
            dve.sem_inc(k32_free, 2)
            dve.sem_inc(V_ev, VCR)
            dve.sem_inc(R_ev, 1)
            dve.sem_inc(rs_chain, 1)
            dve.wait_ge(ln_lo, 4)
            with dve.Fori(0, NB) as b:
                dve.wait_ge(xc_free, b + 1)
                dve.tensor_copy(xch[:], xTh[:, :, bass.ds(b * SEQ, SEQ)].bitcast(F32))
                dve.tensor_copy(xcl[:], xTl[:, :, bass.ds(b * SEQ, SEQ)].bitcast(F32)).then_inc(xc_rdy, 1)
                dve.wait_ge(att_in, b * 16 + 16)
                dve.tensor_scalar(neg[:], attend[0:1, :], 1.0, 1.6e31, ALU.subtract, ALU.mult).then_inc(neg_rdy, 1)
                dve.tensor_reduce(valid[:], attend, AX.X, ALU.max).then_inc(valid_rdy, 1)
                dve.wait_ge(valid_rdy, b + 1)
                dve.sem_inc(att_free, 1)
                for st in range(2):
                    def klo(n):
                        w = MCH[n % 4][1]
                        dve.wait_ge(K_ev, b * 8 + (n + 1))
                        dve.tensor_tensor(kl[:, n % 2, 0:w], k32[:, n % 2, 0:w], kh[:, n % 2, 0:w].bitcast(F32), ALU.subtract).then_inc(kl_rdy, 1)
                        dve.wait_ge(kl_rdy, b * 8 + (n + 1))
                        dve.sem_inc(k32_free, 1)

                    def ptl(g):
                        dve.wait_ge(pTh_rdy, b * 8 + (4 * st + g + 1))
                        if g < 3:
                            dve.tensor_tensor(pTl[:, 4 * g:4 * g + 4, :], ps[:, 4 + g % 2, :].rearrange("p (m s) -> p m s", s=P),
                                              pTh[:, 4 * g:4 * g + 4, :].bitcast(F32), ALU.subtract).then_inc(pTl_rdy, 1)
                        else:
                            dve.tensor_tensor(pTl[0:TAIL, MT - 1, :], ps[0:TAIL, 5, 0:P], pTh[0:TAIL, MT - 1, :].bitcast(F32), ALU.subtract).then_inc(pTl_rdy, 1)

                    dve.wait_ge(S_rdy, b * 2 + (st + 1))
                    dve.tensor_reduce(rmax[:], psf[:, 0:MP], AX.X, ALU.max).then_inc(max_rdy, 1)
                    dve.wait_ge(max_rdy, b * 2 + (st + 1))
                    dve.tensor_scalar(nmax[:], rmax[:], -1.0 / 16, None, ALU.mult).then_inc(nmax_rdy, 1)
                    klo(4 * st)
                    dve.wait_ge(exp_rdy, b * 2 + (st + 1))
                    dve.reciprocal(rsum[:], psum_[:]).then_inc(rsum_rdy, 1)
                    klo(4 * st + 1)
                    dve.wait_ge(rsum_rdy, b * 2 + (st + 1))
                    dve.tensor_tensor(rscale[:], rsum[:], valid[:], ALU.mult).then_inc(rscale_rdy, 1)
                    ptl(0)
                    ptl(1)
                    klo(4 * st + 2)
                    klo(4 * st + 3)
                    ptl(2)
                    ptl(3)

                    def vpart(n):
                        m0, cnt = VUNITS[n]
                        rows = TAIL if m0 == MT - 1 else P
                        return rows, m0, cnt

                    for n in range(4 * st, 4 * st + 4):
                        rows, m0, cnt = vpart(n)
                        dve.wait_ge(V_rdy, b * 8 + (n + 1))
                        dve.tensor_tensor(v32[0:rows, n % 2, 0:cnt, :], ps[0:rows, 6 + n % 2, 0:cnt * D].rearrange("p (i d) -> p i d", d=D),
                                          bv[0:rows, :].unsqueeze(1).broadcast_to([rows, cnt, D]), ALU.add).then_inc(V_ev, 1)
                        dve.wait_ge(vh_rdy, b * 8 + (n + 1))
                        for i in range(cnt):
                            l = dve.tensor_tensor(vstk[0:rows, :, m0 + i, PR:2 * PR], v32[0:rows, n % 2, i, :].rearrange("p (t r) -> p t r", r=PR),
                                                  vstk[0:rows, :, m0 + i, 0:PR].bitcast(F32), ALU.subtract)
                        l.then_inc(vl_rdy, 1)
                    dve.wait_ge(R_rdy, b * 2 + (st + 2))
                    dve.wait_ge(rscale_rdy, b * 2 + (st + 1))
                    x = resid[:, bass.ds(b * 2 + st, 1), :].rearrange("p o d -> p (o d)")
                    dve.scalar_tensor_tensor(out=x, in0=ps[:, 0, 0:D], scalar=rscale[:], in1=x, op0=ALU.mult, op1=ALU.add).then_inc(R_ev, 1)
            dve.wait_ge(R_ev, 2 * NB + 1)
            if stop == "A":
                dve.sem_inc(out_go, 1)
                return

            def ffn(f):
                n, c0, sh, ex, e0 = f["n"], f["c0"], f["sh"], f["ex"], f["e0"]
                ln_front(f["ln"])
                dve.wait_ge(gate_in, 64 * (n + 1))
                dve.tensor_copy(gwh[:], gw_raw[:]).then_inc(gwh_rdy, 1)
                dve.wait_ge(gwh_rdy, n + 1)
                dve.tensor_tensor(gwl[:], gw_raw[:], gwh[:].bitcast(F32), ALU.subtract).then_inc(gw_rdy, 1)
                ln_back(f["ln"])

                seen = [GC[n][0]]

                def link(ins):
                    seen[0] += 1
                    ins.then_inc(g_chain, 1)
                    dve.wait_ge(g_chain, seen[0])

                bias = gb[:].unsqueeze(1).broadcast_to([P, NT, E])
                if n == 0:
                    dve.wait_ge(g_act, 1)
                    link(dve.tensor_tensor(g_c[:], g_s[:], bias, ALU.add))
                    v = g_c[:].rearrange("p t (g e) -> p (t g) e", e=4)
                    dve.tensor_tensor(g_pair[:, :, 0:3], v[:, :, 0:3], v[:, :, 1:4], ALU.add)
                    dve.tensor_tensor(g_pair[:, :, 3:5], v[:, :, 0:2], v[:, :, 2:4], ALU.add)
                    link(dve.tensor_tensor(g_pair[:, :, 5:6], v[:, :, 0:1], v[:, :, 3:4], ALU.add))
                    link(dve.tensor_reduce(g_gs[:], g_pair[:], AX.X, ALU.max))
                    rank(link, g_gs[:].rearrange("p (t g) -> p t g", g=4), g_gr[:], tri4, 4)
                    link(dve.tensor_scalar(g_gr[:], g_gr[:], 2.0, None, ALU.is_lt))
                    link(dve.tensor_tensor(g_c[:].rearrange("p t (g e) -> p (t g) e", e=4), v, g_gr[:].unsqueeze(2).broadcast_to([P, NT * 4, 4]), ALU.mult))
                    top, scale = 6.0, 2.5
                else:
                    lg = ps[:, 4, 0:NT * E].rearrange("p (t e) -> p t e", e=E)
                    dve.wait_ge(L_rdy, 2)
                    link(dve.tensor_reduce(g_t[:], lg, AX.X, ALU.max))
                    link(dve.tensor_tensor(g_c[:], lg, g_t[:].unsqueeze(2).broadcast_to([P, NT, E]), ALU.subtract))
                    assert seen[0] == GC[1][1]
                    dve.wait_ge(g_act, 2)
                    link(dve.tensor_reduce(g_t[:], g_s[:], AX.X, ALU.add))
                    link(dve.reciprocal(g_r[:], g_t[:]))
                    link(dve.tensor_tensor(g_s[:], g_s[:], g_r[:].unsqueeze(2).broadcast_to([P, NT, E]), ALU.mult))
                    link(dve.tensor_tensor(g_c[:], lg, bias, ALU.add))
                    top, scale = 2.0, None
                rank(link, g_c[:], g_rank[:].rearrange("p t e -> p (t e)"), tri16, E)
                link(dve.tensor_scalar(g_rank[:], g_rank[:], top, None, ALU.is_lt))
                link(dve.tensor_tensor(g_w[:], g_rank[:], g_s[:], ALU.mult))
                link(dve.tensor_reduce(g_t[:], g_w[:], AX.X, ALU.add))
                if n == 0:
                    link(dve.tensor_scalar(g_t[:], g_t[:], 1e-20, None, ALU.add))
                link(dve.reciprocal(g_r[:], g_t[:]))
                link(dve.tensor_tensor(g_w[:], g_w[:], g_r[:].unsqueeze(2).broadcast_to([P, NT, E]), ALU.mult))
                if n == 0:
                    link(dve.tensor_scalar(g_w[:], g_w[:], scale, None, ALU.mult))
                assert seen[0] == GC[n][-1], (n, seen[0])
                dve.wait_ge(combh_rdy, n + 1)
                dve.tensor_tensor(combl[:].rearrange("e (b s) -> e b s", b=2), ps[0:E, 5:7, :], combh[:].bitcast(F32).rearrange("e (b s) -> e b s", b=2), ALU.subtract).then_inc(combl_rdy, 1)

                def split(tn, slot, cnt):
                    dve.wait_ge(w_in[slot], cnt)
                    dve.wait_ge(w_free, tn)
                    dve.tensor_copy(w_hi[:, slot, :], w_raw[:, slot, :]).then_inc(w_hi_rdy, 1)
                    dve.wait_ge(w_hi_rdy, tn)
                    dve.tensor_tensor(w_lo[:, slot, :], w_raw[:, slot, 0:3 * D], w_hi[:, slot, 0:3 * D].bitcast(F32), ALU.subtract).then_inc(w_rdy, 1)
                    dve.wait_ge(w_rdy, tn)
                    dve.sem_inc(wraw_free, 1)

                def chunk(ct, half, exp, ec):
                    dve.wait_ge(silu_rdy, ct + 1)
                    dve.wait_ge(U_rdy, ct + 1)
                    dve.tensor_tensor(h32[:, half, :], silu[:, half, :], ps[:, 5, :], ALU.mult).then_inc(mul1_rdy, 1)
                    if exp:
                        dve.wait_ge(mul1_rdy, ct + 1)
                        dve.wait_ge(C_rdy, ec)
                        dve.tensor_tensor(h32[:, half, :], h32[:, half, :], ps[:, 6, :], ALU.mult).then_inc(mul2_rdy, 1)
                    dve.wait_ge(hh_rdy, ct + 1)
                    dve.tensor_tensor(hl[:, half, :], h32[:, half, :], hh[:, half, :].bitcast(F32), ALU.subtract).then_inc(hl_rdy, 1)

                t0 = f["t0"]
                split(t0 + 1, t0 % 2, 16 * (t0 // 2 + 1))
                split(t0 + 2, (t0 + 1) % 2, 16 * ((t0 + 1) // 2 + 1))
                for k in range(sh):
                    for half in range(2):
                        chunk(c0 + 2 * k + half, half, False, None)
                    if k >= 1:
                        tn = t0 + k + 1
                        split(tn + 1, tn % 2, 16 * (tn // 2 + 1))
                tb = t0 + sh
                def pair(i, last):
                    for j in range(2):
                        for half in range(2):
                            chunk(i * 4 + (c0 + 2 * sh + 2 * j + half), half, True, i * 4 + (e0 + 2 * j + half + 1))
                            if half == 0 and not (last and j == 1):
                                tn = tb + j + 1
                                split(i * 2 + (tn + 1), tn % 2, i * 16 + 16 * (tn // 2 + 1))
                with dve.Fori(0, ex // 2 - 1) as i:
                    pair(i, False)
                pair(ex // 2 - 1, True)
                dve.wait_ge(down_done, 2 * (t0 + sh + ex))
                for q in range(4):
                    x = resid[:, 2 * q:2 * q + 2, :].rearrange("p t d -> p (t d)")
                    dve.tensor_tensor(x, x, ps[:, q, :], ALU.add).then_inc(add_rdy, 1)
                dve.wait_ge(add_rdy, 4 * (n + 1))

            dve.sem_inc(wraw_free, 2)
            ffn(FFN["B"])
            if stop == "B":
                dve.sem_inc(out_go, 1)
                return

            ln_front(2)
            dve.wait_ge(cw_in, 16 * 16)
            for r, h in ((wq_raw[:], wqh[:]), (wo_raw[:], woh[:])):
                dve.tensor_copy(h, r).then_inc(cwh, 1)
            dve.wait_ge(cwh, 2)
            for r, h, l in ((wq_raw[:], wqh[:], wql[:]), (wo_raw[:], woh[:], wol[:])):
                dve.tensor_tensor(l.rearrange("p a b c -> p (a b c)") if len(l.shape) == 4 else l, r.rearrange("p a b c -> p (a b c)") if len(l.shape) == 4 else r,
                                  (h.rearrange("p a b c -> p (a b c)") if len(l.shape) == 4 else h).bitcast(F32), ALU.subtract).then_inc(cw_rdy, 2)
            for h in range(2):
                q = dve.tensor_scalar(bqm[0:96, h, :], bq[0:96, :], hmask[0:96, h:h + 1], None, ALU.mult)
            q.then_inc(bq_rdy, 1)
            dve.tensor_scalar(rs[:], rs[:], 0.0, 0.3, ALU.max, ALU.min).then_inc(bq_rdy, 1)
            dve.wait_ge(bq_rdy, 2)
            dve.memset(qs[96:97, :, :, :].bitcast(F32), 1.0).then_inc(q_set, 1)
            ln_back(2)
            for n in range(2 * NPAIR):
                t, half = n // 2, n % 2
                dve.wait_ge(q_32, 2 * n + 2)
                for h in range(2):
                    src = ps[0:3 * PR, 4 + n % 4, :].rearrange("p (b s) -> p b s", b=2)
                    dst = qs[0:3 * PR, :, h, :].rearrange("p (b t) s -> p b t s", t=NPAIR)[:, 2 * half:2 * half + 2, t, :]
                    dve.tensor_scalar(dst, src, hmask[0:96, h:h + 1], bqm[0:96, h, t:t + 1], ALU.mult, ALU.add).then_inc(q_hi, 1)
                    dve.wait_ge(q_hi, 2 * n + h + 1)
                    lo = qs[2 * PR:3 * PR, :, h, :].rearrange("p (b t) s -> p b t s", t=NPAIR)[:, 2 * half:2 * half + 2, t, :]
                    dve.tensor_tensor(lo, q32[2 * PR:3 * PR, h, :].rearrange("p (b s) -> p b s", b=2), lo.bitcast(F32), ALU.subtract).then_inc(q_lo, 1)

            dve.sem_inc(pl_free, 3)
            dve.sem_inc(cx_rdy, 1)

            def clip(i, u, c):
                g = i * (2 * NCH) + (u * NCH + c)
                rows, w = (P, 1024) if c < NCH - 1 else (TAIL, 512)
                t = p32[0:rows, PSLOT[c], 0:w]
                dve.wait_ge(p_exp, g + 1 + 2)
                dve.tensor_scalar(t, t, CLO, CHI, ALU.max, ALU.min).then_inc(p_clip, 1)

            def low(i, u, c):
                g = i * (2 * NCH) + (u * NCH + c)
                rows, w = (P, 1024) if c < NCH - 1 else (TAIL, 512)
                buf = (u * NCH + c) % 2
                dve.wait_ge(ph_rdy, g + 1)
                dve.wait_ge(pv_done, g + 1)
                dve.tensor_tensor(pl[0:rows, buf, 0:w], p32[0:rows, PSLOT[c], 0:w], ph[0:rows, buf, 0:w].bitcast(F32), ALU.subtract).then_inc(pl_rdy, 1)
                dve.wait_ge(pl_rdy, g + 1)
                dve.sem_inc(pl_free, 1)

            def norm(i, u):
                job = i * 2 + u
                T = ps[:, 6, 0:128].rearrange("p (q c) -> p q c", c=32)
                dve.wait_ge(osum_rdy, job + 1)
                dve.tensor_scalar(s4[:, u, :], T[:, :, HD], 1.0 + 1e-8, None, ALU.mult).then_inc(s4_rdy, 1)
                dve.wait_ge(s4_rdy, job + 1)
                dve.reciprocal(r4[:, u, :], s4[:, u, :]).then_inc(r4_rdy, 1)
                dve.wait_ge(r4_rdy, job + 1)
                o = cx[:, :, bass.ds(job, 1), :].rearrange("p s o (h r) -> p h (s o) r", h=2)
                dve.tensor_tensor(o, T[:, :, 0:HD].rearrange("p (h s) r -> p h s r", h=2),
                                  r4[:, u, :].rearrange("p (h s) -> p h s", h=2).unsqueeze(3).broadcast_to([P, 2, 2, HD]), ALU.mult).then_inc(cx_rdy, 1)

            def job_pair(i, first, last):
                for x in range(2 * NCH):
                    y = x + 1
                    if y < 2 * NCH:
                        clip(i, y // NCH, y % NCH)
                    elif not last:
                        clip(i + 1, 0, 0)
                    if x == 4 and not first:
                        norm(i - 1, 1)
                    if x == NCH + 4:
                        norm(i, 0)
                    low(i, x // NCH, x % NCH)

            clip(0, 0, 0)
            job_pair(0, True, False)
            with dve.Fori(1, NJ // 2 - 1) as i:
                job_pair(i, False, False)
            job_pair(NJ // 2 - 1, False, True)
            norm(NJ // 2 - 1, 1)
            for q in range(4):
                dve.wait_ge(cTh_rdy, q + 1)
                dve.tensor_tensor(cTxl[:, q, :], ps[:, q, :], cTxh[:, q, :].bitcast(F32), ALU.subtract).then_inc(cTl_rdy, 1)
            k = [0]

            def chain(ins):
                k[0] += 1
                ins.then_inc(dl_a, 1)

            for q in range(4):
                dve.wait_ge(dl_rdy, q + 1)
                chain(dve.tensor_tensor(dlt[:, 2 * q:2 * q + 2, :], ps[:, 4 + q, :].rearrange("p (t d) -> p t d", t=2), bo[:].unsqueeze(1).broadcast_to([P, 2, D]), ALU.add))
            dve.wait_ge(dl_a, k[0])
            d2 = dlt[:].rearrange("p t d -> p (t d)")
            chain(dve.tensor_scalar(d2, d2, rs[:], None, ALU.mult))
            dve.wait_ge(dl_a, k[0])
            for t in range(NT):
                chain(dve.bn_stats(st6[:, t, :], dlt[:, t, :]))
            dve.wait_ge(dl_a, k[0])
            for t in range(NT):
                chain(dve.bn_aggr(mv[:, t, :], st6[:, t, :]))
            assert k[0] == DLA
            dve.wait_ge(dl_std, 1)
            dve.reciprocal(rstd[:], std[:]).then_inc(dl_b, 1)
            dve.wait_ge(dl_b, 1)
            for t in range(NT):
                dve.tensor_scalar(dlt[:, t, :], dlt[:, t, :], mv[:, t, 0:1], rstd[:, t:t + 1], ALU.subtract, ALU.mult).then_inc(dl_b, 1)
            gb8, bb8 = (z[:].unsqueeze(1).broadcast_to([P, NT, D]) for z in (gam, bet))
            for n_, (in1, op) in enumerate(((gb8, ALU.mult), (bb8, ALU.add))):
                dve.wait_ge(dl_b, 9 + n_)
                dve.tensor_tensor(dlt[:], dlt[:], in1, op).then_inc(dl_b, 1)
            dve.wait_ge(dl_b, 11)
            dve.tensor_tensor(resid[:], resid[:], dlt[:], ALU.add).then_inc(dl_b, 1)
            dve.wait_ge(dl_b, 12)
            if stop == "C":
                dve.sem_inc(out_go, 1)
                return
            ffn(FFN["D"])
            dve.sem_inc(out_go, 1)


def kernel(**inp):
    import concourse.bacc as bacc
    from concourse.bass_utils import run_bass_kernel_spmd

    get = lambda n: np.ascontiguousarray(inp[n])
    g0, u0, d0 = get("L0_ffn_gate_proj"), get("L0_ffn_up_proj"), get("L0_ffn_down_proj")
    ex0 = [g0.reshape(E * I0, D), u0.reshape(E * I0, D), d0.transpose(0, 2, 1).reshape(E * I0, D)]
    sh0 = [get("L0_ffn_shared_gate_w"), get("L0_ffn_shared_up_w"), get("L0_ffn_shared_down_w").T]
    ex1 = [get("L1_ffn_Wu").transpose(0, 2, 1).reshape(E * I1, D), get("L1_ffn_Wg").transpose(0, 2, 1).reshape(E * I1, D),
           get("L1_ffn_Wd").reshape(E * I1, D)]
    sh1 = [get("L1_ffn_Su")[0].T, get("L1_ffn_Sg")[0].T, get("L1_ffn_Sd")[0]]

    def pack(shared, experts, width):
        pad = -len(shared[0]) % P
        g, u, d = (np.concatenate([np.pad(s, ((0, pad), (0, 0))), e]) for s, e in zip(shared, experts))
        n = len(g) // P
        first = (len(shared[0]) + pad) // P
        sel = np.zeros((n, P, P), np.float32)
        for r in range(E * width):
            sel[first + r // P, r // width, r % P] = 1.0
        col = lambda w: w.reshape(n, P, KT, P).transpose(0, 3, 2, 1).reshape(n, P, D)
        return np.ascontiguousarray(np.concatenate([col(g), col(u), d.reshape(n, P, D), sel], axis=2))

    c = get("ctx_2048")
    tr = lambda n: np.ascontiguousarray(get(n).T)
    row = np.arange(P)[:, None]
    msum = np.zeros((VC, 2, HD + 1), np.float32)
    for h in range(2):
        for r in range(HD):
            msum[h * HD + r, h, r] = msum[PR + h * HD + r, h, r] = 1.0
        msum[2 * PR, h, HD] = 1.0
    before = lambda w: np.tile(np.tril(np.ones((w, w), np.float32), -1).reshape(1, w * w), (P, 1))
    arrays = {
        "x": get("x").reshape(NB * SEQ, D),
        "ctxT": np.ascontiguousarray(np.pad(c.transpose(0, 2, 1), ((0, 0), (0, 0), (0, MP - M))).reshape(NB * KT, P, MP)),
        "ctxN": np.pad(c, ((0, 0), (0, MT * P - M), (0, 0))),
        "attend": np.pad(get("mask_BxS2_bk0").view(np.uint8), ((0, 0), (0, 4 * MW - M))).view(np.int32),
        "keep": np.pad(get("mask_BxS2_ik0"), ((0, 0), (0, MP - M))),
        "wqT": tr("L1_xattn_Wq"), "wkT": tr("L1_xattn_Wk"), "wvT": tr("L1_xattn_Wv"), "woT": tr("L1_xattn_Wo"),
        "bq": get("L1_xattn_bq").reshape(NPAIR, PR).T, "bk": get("L1_xattn_bk").reshape(KT, P).T, "bv": get("L1_xattn_bv"), "bo": get("L1_xattn_bo"),
        "gam": get("L1_xattn_ln_gamma"), "bet": get("L1_xattn_ln_beta"), "rs": get("L1_xattn_residual_scale").reshape(1),
        "gw0": tr("L0_ffn_gate_weight"), "gb0": get("L0_ffn_e_score_correction_bias"),
        "gw1": tr("L1_ffn_router_w"), "gb1": get("L1_ffn_router_bias"),
        "w0": pack(sh0, ex0, I0), "w1": pack(sh1, ex1, I1),
        "ident": np.eye(P, dtype=np.float32), "tri16": before(E), "tri4": before(4), "msum": msum,
        "hmask": ((row % PR) // HD == np.arange(2)[None, :]).astype(np.float32),
    }
    nc = bacc.Bacc("TRN2", target_bir_lowering=False, num_devices=1)
    sent, a = {}, {}
    for name, v in arrays.items():
        v = np.ascontiguousarray(v)
        sent[f"in_{name}"] = v
        a[name] = nc.dram_tensor(f"in_{name}", v.shape, mybir.dt.from_np(v.dtype), kind="ExternalInput").ap()
    out = nc.dram_tensor("out_0", (NB * SEQ, D), F32, kind="ExternalOutput").ap()
    build(nc, a, out, STOP)
    r = run_bass_kernel_spmd(nc, [sent], core_ids=[0])
    return r.results[0]["out_0"].reshape(NB, SEQ, D)


STOP = "D"
```

```python
from contextlib import ExitStack

import numpy as np
import concourse.bass as bass
from concourse import mybir

F32 = mybir.dt.float32
F32R = mybir.dt.float32r
U8 = mybir.dt.uint8
I32 = mybir.dt.int32
ALU = mybir.AluOpType
ACT = mybir.ActivationFunctionType
AX = mybir.AxisListType

P = 128
NB, SEQ, D = 4, 256, 256
NT = NB * SEQ // P
KT = D // P
M = 1601
MP = M + M % 2
MW = -(-M // 4)
MT = -(-M // P)
TAIL = M - (MT - 1) * P
MCH = [(c * 512, min(512, MP - c * 512)) for c in range(-(-MP // 512))]
NH, HD = 16, 16
NPAIR = NH // 2
PR = 2 * HD
NJ = NB * NPAIR
VC = 2 * PR + 1
QROWS = 3 * PR + 1
E = 16
I0, SH0 = 176, 352
I1, SH1 = 128, 256
NSH0 = -(-SH0 // P)
NEX0 = E * I0 // P
NSH1 = SH1 // P
NEX1 = E * I1 // P
WC = 3 * D + P
EPS = 1e-5
CLO, CHI = float(np.exp(-50.0)), float(np.exp(50.0))
VUNITS = [(0, 2), (2, 2), (4, 2), (6, 2), (8, 2), (10, 1), (11, 1), (12, 1)]
PIECES = [("t", 0, 0, 1024), ("t", 1, 0, 1024), ("t", 0, 1024, MP - 1024), ("t", 1, 1024, MP - 1024),
          ("n", 0, 0, 4), ("n", 0, 4, 4), ("n", 0, 8, 4), ("n", 0, 12, 1)]
NP_ = len(PIECES)
NCH = 7
IT = 2 * NCH
HI_LAG, LO_LAG, PV_LAG = 1, 2, 3
EVAC_LAG, OSUM_LAG, NORM_LAG = (NCH + PV_LAG + n for n in range(3))
DRAIN = IT + PV_LAG + 3
NPOOL = NCH // 2
NATIVE = (1, 3)
CR_SC = NCH + 1
CR_PV = 2 * NCH + 3
GC = [(0, 20), (20, 22, 35)]
DLA = 4 + 2 * NT
CROWS = 32 + E
VCR = 3
CR_VR = 1


def build(nc, a, out, stop="D"):
    kh_d = nc.dram_tensor("k_hi", [NB * D, MP], F32).ap()
    kl_d = nc.dram_tensor("k_lo", [NB * D, MP], F32).ap()
    v_d = nc.dram_tensor("v_stack", [NJ, P, MT * VC], F32).ap()
    m_d = nc.dram_tensor("key_mask", [NJ, MP], F32).ap()

    with ExitStack() as ctx:
        def sbuf(stack, name, shape, dt=F32):
            return stack.enter_context(nc.sbuf_tensor(name, shape, dt))

        sb = lambda name, shape, dt=F32: sbuf(ctx, name, shape, dt)
        sem = lambda name: ctx.enter_context(nc.semaphore(name))

        resid = sb("resid", [P, NT, D])
        xn = sb("xn", [P, NT, D])
        xTh = sb("xTh", [P, KT, NT * P], F32R)
        xTl = sb("xTl", [P, KT, NT * P], F32R)
        st6 = sb("st6", [P, NT, 6])
        mv = sb("mv", [P, NT, 2])
        std = sb("std", [P, NT])
        rstd = sb("rstd", [P, NT])
        eps = sb("eps", [P, 1])
        ident = sb("ident", [P, P])
        zero = sb("zero", [P, P], F32R)
        one_row = sb("one_row", [1, P], F32R)
        with ExitStack() as s:
            A = lambda name, shape, dt=F32: sbuf(s, name, shape, dt)
            raw = A("raw", [P, 2, 1024])
            cTh, cTl = A("cTh", [P, 2, KT, MP], F32R), A("cTl", [P, 2, KT, MP], F32R)
            cNh, cNl = A("cNh", [P, MT, D], F32R), A("cNl", [P, MT, D], F32R)
            with ExitStack() as sw:
                wk_raw, wv_raw = (sbuf(sw, n, [P, KT, D]) for n in ("wk_raw", "wv_raw"))
            prob = A("prob", [P, MP])
            wkh, wkl = A("wkh", [P, KT, D], F32R), A("wkl", [P, KT, D], F32R)
            wvh, wvl = A("wvh", [P, KT, D], F32R), A("wvl", [P, KT, D], F32R)
            bk = A("bk", [P, KT])
            bv = A("bv", [P, D])
            xch, xcl = A("xch", [P, KT, SEQ], F32R), A("xcl", [P, KT, SEQ], F32R)
            attend_w = A("attend", [P, MW], I32)
            attend = attend_w[:].bitcast(U8)[:, 0:MP]
            neg = A("neg", [1, MP], F32R)
            valid = A("valid", [P, 1])
            mi = A("mi", [NPAIR, MP], I32)
            mneg = mi[:].bitcast(F32)
            nmax = A("nmax", [P, 1])
            rmax = A("rmax", [P, 1])
            psum_ = A("psum_", [P, 1])
            rsum = A("rsum", [P, 1])
            rscale = A("rscale", [P, 1])
            pTh, pTl = A("pTh", [P, MT, P], F32R), A("pTl", [P, MT, P], F32R)
            k32 = A("k32", [P, 2, 512])
            kh, kl = A("kh", [P, 2, 512], F32R), A("kl", [P, 2, 512], F32R)
            v32 = A("v32", [P, 2, 2, D])
            vstk = A("vstk", [P, NPAIR, MT, VC], F32R)
        with ExitStack() as s:
            Bt = lambda name, shape, dt=F32: sbuf(s, name, shape, dt)
            w_raw = Bt("w_raw", [P, 2, WC])
            gw_raw = Bt("gw_raw", [P, KT, E])
            gb = Bt("gb", [P, E])
            tri16 = Bt("tri16", [P, E * E])
            tri4 = Bt("tri4", [P, 16])
            gwh, gwl = Bt("gwh", [P, KT, E], F32R), Bt("gwl", [P, KT, E], F32R)
            w_hi = Bt("w_hi", [P, 2, WC], F32R)
            w_lo = Bt("w_lo", [P, 2, 3 * D], F32R)
            silu = Bt("silu", [P, 2, 512])
            h32 = Bt("h32", [P, 2, 512])
            hh, hl = Bt("hh", [P, 2, 512], F32R), Bt("hl", [P, 2, 512], F32R)
            logit = Bt("logit", [E, NT * P])
            comb = Bt("comb", [CROWS, NT * P], F32R)
            g_s = Bt("g_s", [P, NT, E])
            g_c = Bt("g_c", [P, NT, E])
            g_pair = Bt("g_pair", [P, NT * 4, 6])
            g_gs = Bt("g_gs", [P, NT * 4])
            g_gr = Bt("g_gr", [P, NT * 4])
            g_big = Bt("g_big", [P, NT * E, E])
            g_eq = Bt("g_eq", [P, NT * E, E])
            g_rank = Bt("g_rank", [P, NT, E])
            g_w = Bt("g_w", [P, NT, E])
            g_t = Bt("g_t", [P, NT])
            g_r = Bt("g_r", [P, NT])
        with ExitStack() as s:
            C = lambda name, shape, dt=F32: sbuf(s, name, shape, dt)
            qs = C("qs", [P, NJ, 2, SEQ], F32R)
            kslot = C("kslot", [P, 2, MP], F32R)
            vslot = C("vslot", [P, 2, MT * VC], F32R)
            oT = C("oT", [VC, 2, 512])
            cx = C("cx", [P, 2, NJ, PR])
            wo_raw = C("wo_raw", [P, KT, D])
            woh, wol = C("woh", [P, KT, D], F32R), C("wol", [P, KT, D], F32R)
            bq = C("bq", [P, NPAIR])
            hmask = C("hmask", [P, 2])
            bo = C("bo", [P, D])
            gam, bet = C("gam", [P, D]), C("bet", [P, D])
            rs = C("rs", [P, 1])
            msum = C("msum", [VC, 2, HD + 1])
            s4 = C("s4", [P, 2, 4])
            r4 = C("r4", [P, 2, 4])
            with ExitStack() as sq:
                wq_raw = sbuf(sq, "wq_raw", [P, KT, NPAIR, 3 * PR])
                wqh, wql = (sbuf(sq, n, [P, KT, NPAIR, 3 * PR], F32R) for n in ("wqh", "wql"))
                q32 = sbuf(sq, "q32", [P, 4, 512])
            with ExitStack() as sq:
                p32 = sbuf(sq, "p32", [P, NCH, 1024])
            pl = C("pl", [P, NCH, 1024], F32R)
            ph = C("ph", [P, NCH, 1024], F32R)
        cTxh, cTxl = (t[:].rearrange("p k n -> p (k n)").rearrange("p (q n) -> p q n", n=512) for t in (xTh, xTl))
        dlt = xn

        ps = ctx.enter_context(nc.psum_tensor("ps", [P, 8, 512], F32))
        psf = ps[:, :, :].rearrange("p b n -> p (b n)")

        x_in, wkv_in, cst_in, gate_in, cw_in = sem("x_in"), sem("wkv_in"), sem("cst_in"), sem("gate_in"), sem("cw_in")
        cst_set, vstk_set, first_hi = sem("cst_set"), sem("vstk_set"), sem("first_hi")
        wkv_hi, wkv_rdy = sem("wkv_hi"), sem("wkv_rdy")
        ln_stat, ln_mv, ln_std, ln_rstd, ln_xn = (sem(n) for n in ("ln_stat", "ln_mv", "ln_std", "ln_rstd", "ln_xn"))
        ln_T, ln_hi, ln_lo = sem("ln_T"), sem("ln_hi"), sem("ln_lo")
        raw_in = [sem("raw_in0"), sem("raw_in1")]
        raw_free, split_hi = sem("raw_free"), sem("split_hi")
        ctxT_rdy, ctxN_hi, ctxN_rdy = sem("ctxT_rdy"), sem("ctxN_hi"), sem("ctxN_rdy")
        att_in, att_free, mi_in = sem("att_in"), sem("att_free"), sem("mi_in")
        mneg_rdy, md_out = sem("mneg_rdy"), sem("md_out")
        neg_rdy, xc_rdy = sem("neg_rdy"), sem("xc_rdy")
        S_rdy, max_rdy, nmax_rdy, exp_rdy = sem("S_rdy"), sem("max_rdy"), sem("nmax_rdy"), sem("exp_rdy")
        K_rdy, K_ev, k32_rdy, kl_rdy, k32_free = sem("K_rdy"), sem("K_ev"), sem("k32_rdy"), sem("kl_rdy"), sem("k32_free")
        k_out = [sem("k_out0"), sem("k_out1")]
        V_rdy, V_ev, vh_rdy, vl_rdy = sem("V_rdy"), sem("V_ev"), sem("vh_rdy"), sem("vl_rdy")
        v_out = sem("v_out")
        T_rdy, pTh_rdy, pTl_rdy = sem("T_rdy"), sem("pTh_rdy"), sem("pTl_rdy")
        R_rdy, R_ev, rs_chain = sem("R_rdy"), sem("R_ev"), sem("rs_chain")
        w_in = [sem("w_in0"), sem("w_in1")]
        w_hi_rdy, w_rdy = sem("w_hi_rdy"), sem("w_rdy")
        G_rdy, U_rdy, silu_rdy, mul1_rdy = sem("G_rdy"), sem("U_rdy"), sem("silu_rdy"), sem("mul1_rdy")
        C_rdy, mul2_rdy, hh_rdy, hl_rdy, down_done = sem("C_rdy"), sem("mul2_rdy"), sem("hh_rdy"), sem("hl_rdy"), sem("down_done")
        gwh_rdy, gw_rdy, L_rdy, g_act, g_chain = sem("gwh_rdy"), sem("gw_rdy"), sem("L_rdy"), sem("g_act"), sem("g_chain")
        LT_rdy, LT_ev, comb_set, gT_rdy, combh_rdy, combl_rdy = sem("LT_rdy"), sem("LT_ev"), sem("comb_set"), sem("gT_rdy"), sem("combh_rdy"), sem("combl_rdy")
        add_rdy = sem("add_rdy")
        cwh, cw_rdy, bq_rdy = sem("cwh"), sem("cw_rdy"), sem("bq_rdy")
        Q_rdy, q_hi0, q_hi, q_32, q_lo = sem("Q_rdy"), sem("q_hi0"), sem("q_hi"), sem("q_32"), sem("q_lo")
        kv_in = [sem("kv_in0"), sem("kv_in1")]
        sc_rdy, p_exp, p_clip, ph_rdy, pl_rdy, pv_done = (sem(n) for n in ("sc_rdy", "p_exp", "p_clip", "ph_rdy", "pl_rdy", "pv_done"))
        pool_ph, pool_pl = sem("pool_ph"), sem("pool_pl")
        oT_rdy, osum_rdy, s4_rdy, r4_rdy, cx_rdy = (sem(n) for n in ("oT_rdy", "osum_rdy", "s4_rdy", "r4_rdy", "cx_rdy"))
        cT_rdy, cTh_rdy, cTl_rdy, dl_rdy, dl_a, dl_std, dl_b, beta_rdy = (sem(n) for n in ("cT_rdy", "cTh_rdy", "cTl_rdy", "dl_rdy", "dl_a", "dl_std", "dl_b", "beta_rdy"))
        pool_go = sem("pool_go")
        out_done, out_go = sem("out_done"), sem("out_go")
        valid_rdy, rsum_rdy, rscale_rdy = sem("valid_rdy"), sem("rsum_rdy"), sem("rscale_rdy")
        q_set, wraw_free = sem("q_set"), sem("wraw_free")

        block = ctx.enter_context(nc.Block())

        def at(y):
            return y // NCH, y % NCH

        def split_part(c):
            return (TAIL if c == NCH - 1 else P), (1024 if c % 2 and c not in NATIVE else 512)

        def alive(i, y, per):
            return not isinstance(i, int) or 0 <= i * per + y < NJ * per // 2

        def q_parts(n, h):
            t, half = n // 2, n % 2
            dst = qs[0:3 * PR, :, h, :].rearrange("p (b t) s -> p b t s", t=NPAIR)[:, 2 * half:2 * half + 2, t, :]
            return dst, q32[0:3 * PR, n % 4, :].rearrange("p (b s) -> p b s", b=2)

        FFN = {"B": dict(w=a["w0"], sh=NSH0, ex=NEX0, t0=0, n=0, ln=1, gw=a["gw0"], gb=a["gb0"]),
               "D": dict(w=a["w1"], sh=NSH1, ex=NEX1, t0=NSH0 + NEX0, n=1, ln=3, gw=a["gw1"], gb=a["gb1"])}
        for f in FFN.values():
            f["c0"] = 2 * f["t0"]
            f["e0"] = 2 * NEX0 * f["n"]
            f["p0"] = f["c0"]

        def store(sp):
            sp.wait_ge(out_go, 1)
            sp.dma_start(out.rearrange("(t p) d -> p t d", p=P), resid[:]).then_inc(out_done, 16)
            sp.wait_ge(out_done, 16)

        @block.sync
        def _(sp):
            sp.dma_start(resid[:], a["x"].rearrange("(t p) d -> p t d", p=P)).then_inc(x_in, 16)
            sp.dma_start(ident[:], a["ident"]).then_inc(cst_in, 16)

            def tile(f, i, k):
                slot = (f["t0"] + k) % 2
                sp.wait_ge(wraw_free, i + (f["t0"] + k + 1))
                sp.dma_start(w_raw[:, slot, :], f["w"][bass.ds(i + k, 1)].rearrange("o p n -> (o p) n")).then_inc(w_in[slot], 16)

            def load_first(f):
                for t, s in ((gw_raw, f["gw"].rearrange("(k p) n -> p k n", p=P)), (gb, f["gb"].rearrange("(o n) -> o n", o=1).broadcast_to([P, E])),
                             (tri16, a["tri16"]), (tri4, a["tri4"])):
                    sp.dma_start(t[:], s).then_inc(gate_in, 16)
                tile(f, 0, 0)
                tile(f, 0, 1)

            def load_rest(f):
                for k in range(2, f["sh"]):
                    tile(f, 0, k)
                with sp.Fori(0, f["ex"] // 2) as i:
                    for j in range(2):
                        tile(f, i * 2, f["sh"] + j)

            def piece(b, n):
                kind, k, c0, w = PIECES[n]
                sp.wait_ge(raw_free, b * NP_ + (n + 1))
                if kind == "t":
                    src = a["ctxT"][bass.ds(b * KT + k, 1), :, c0:c0 + w].rearrange("o p n -> (o p) n")
                    dst = raw[:, n % 2, 0:w]
                else:
                    src = a["ctxN"][bass.ds(b, 1), c0 * P:(c0 + w) * P, :].rearrange("o (t p) d -> p (o t) d", p=P)
                    dst = raw[:, n % 2, 0:w * D].rearrange("p (t d) -> p t d", d=D)
                sp.dma_start(dst, src).then_inc(raw_in[n % 2], 16)

            def masks_in(b):
                sp.wait_ge(att_free, b + 1)
                sp.dma_start(attend_w[:], a["attend"][bass.ds(b, 1), :].broadcast_to([P, MW])).then_inc(att_in, 16)
                sp.wait_ge(md_out, b * 16 + 16)
                sp.dma_start(mi[:], a["keep"][bass.ds(b, 1), :].broadcast_to([NPAIR, MP])).then_inc(mi_in, 16)

            def key_out(b, n):
                mt, (c0, w) = n // 4, MCH[n % 4]
                sp.wait_ge(kl_rdy, b * 8 + (n + 1))
                for t, dr in ((kh, kh_d), (kl, kl_d)):
                    sp.dma_start(dr[bass.ds(b * D + mt * P, P), c0:c0 + w], t[:, n % 2, 0:w].bitcast(F32)).then_inc(k_out[n % 2], 16)

            def batch_io(b, last):
                sp.wait_ge(mneg_rdy, b + 1)
                sp.dma_start(m_d[bass.ds(b * NPAIR, NPAIR), :], mneg).then_inc(md_out, 16)
                piece(b, 4)
                piece(b, 5)
                if not last:
                    masks_in(b + 1)
                for n in range(8):
                    key_out(b, n)
                    if n < 2:
                        piece(b, 6 + n)
                    elif n < 4 and not last:
                        piece(b + 1, 2 * n - 4)
                        piece(b + 1, 2 * n - 3)
                if last and stop != "A":
                    sp.wait_ge(raw_free, NB * NP_ + 2)
                    sp.wait_ge(V_rdy, 8 * NB + CR_VR)
                    load_first(FFN["B"])
                sp.wait_ge(vl_rdy, b * 8 + 8)
                sp.dma_start(v_d[bass.ds(b * NPAIR, NPAIR), :, :].rearrange("t p n -> p t n"),
                             vstk[:].bitcast(F32).rearrange("p t m c -> p t (m c)")).then_inc(v_out, 16)

            piece(0, 0)
            piece(0, 1)
            masks_in(0)
            piece(0, 2)
            piece(0, 3)
            for t, s in ((wk_raw, a["wkT"]), (wv_raw, a["wvT"])):
                sp.dma_start(t[:], s.rearrange("(k p) n -> p k n", p=P)).then_inc(wkv_in, 16)
            sp.dma_start(bk[:], a["bk"]).then_inc(wkv_in, 16)
            sp.dma_start(bv[:], a["bv"].rearrange("(o n) -> o n", o=1).broadcast_to([P, D])).then_inc(wkv_in, 16)
            with sp.Fori(0, NB - 1) as b:
                batch_io(b, False)
            batch_io(NB - 1, True)

            def scratch_out():
                for n in range(2):
                    sp.wait_ge(k_out[n], 32 * (NB * 4 + 1))
                sp.wait_ge(v_out, 16 * (NB + 1))
                sp.wait_ge(md_out, 16 * (NB + 1))

            if stop == "A":
                scratch_out()
                return store(sp)
            sp.wait_ge(ln_stat, 2)
            for r in range(3):
                for k in range(KT):
                    sp.dma_start(wq_raw[:, k, :, PR * r:PR * r + PR], a["wqT"][k * P:(k + 1) * P, :].rearrange("p (t n) -> p t n", n=PR)).then_inc(cw_in, 16)
                sp.dma_start(bq[PR * r:PR * r + PR, :], a["bq"]).then_inc(cw_in, 16)
            for t, s in ((wo_raw[:], a["woT"].rearrange("(k p) n -> p k n", p=P)), (hmask[:], a["hmask"]), (msum[:], a["msum"]),
                         (bo[:], a["bo"].rearrange("(o n) -> o n", o=1).broadcast_to([P, D])),
                         (gam[:], a["gam"].rearrange("(o n) -> o n", o=1).broadcast_to([P, D])),
                         (bet[:], a["bet"].rearrange("(o n) -> o n", o=1).broadcast_to([P, D])),
                         (rs[:], a["rs"].rearrange("(o n) -> o n", o=1).broadcast_to([P, 1]))):
                sp.dma_start(t, s).then_inc(cw_in, 16)
            load_rest(FFN["B"])
            scratch_out()
            if stop == "B":
                return store(sp)

            with sp.Fori(0, NJ // 2) as i:
                for u in range(2):
                    sp.wait_ge(sc_rdy, i * IT + (u * NCH - NCH + CR_SC))
                    rows = bass.ds(i * (2 * PR) + u * PR, PR)
                    for r, dr in enumerate((kh_d, kl_d, kh_d)):
                        sp.dma_start(kslot[PR * r:PR * r + PR, u, :].bitcast(F32), dr[rows, :]).then_inc(kv_in[u], 16)
                    job = bass.ds(i * 2 + u, 1)
                    sp.dma_start(kslot[3 * PR:QROWS, u, :].bitcast(F32), m_d[job, :]).then_inc(kv_in[u], 16)
                    sp.wait_ge(pv_done, i * IT + (u * NCH - NCH + CR_PV))
                    sp.dma_start(vslot[:, u, :].bitcast(F32), v_d[job].rearrange("o p n -> (o p) n")).then_inc(kv_in[u], 16)
            if stop == "C":
                return store(sp)
            sp.wait_ge(sc_rdy, NJ * NCH + CR_SC)
            load_first(FFN["D"])
            load_rest(FFN["D"])
            store(sp)

        @block.gpsimd
        def _(pool):
            pool.memset(zero[:].bitcast(F32), 0.0).then_inc(cst_set, 1)
            pool.memset(one_row[:].bitcast(F32), 1.0).then_inc(cst_set, 1)
            pool.memset(eps[:], EPS).then_inc(cst_set, 1)
            pool.sem_inc(raw_free, 2)
            pool.sem_inc(md_out, 16)
            pool.memset(vstk[:].bitcast(F32), 0.0).then_inc(vstk_set, 1)
            pool.wait_ge(vstk_set, 1)
            pool.memset(vstk[:, :, :, 2 * PR:VC].bitcast(F32), 1.0).then_inc(vstk_set, 1)

            def split_context(i, bb, last):
                for n in range(4, NP_):
                    c0, w = PIECES[n][2:]
                    hi, lo = cNh[:, c0:c0 + w, :], cNl[:, c0:c0 + w, :]
                    src = raw[:, n % 2, 0:w * D].rearrange("p (t d) -> p t d", d=D)
                    pool.wait_ge(ctxN_hi, i * 8 + (4 * bb + n - 4 + 1))
                    pool.tensor_tensor(lo, src, hi.bitcast(F32), ALU.subtract).then_inc(ctxN_rdy, 1)
                    pool.wait_ge(ctxN_rdy, i * 8 + (4 * bb + n - 4 + 1))
                    pool.sem_inc(raw_free, 1)
                if last:
                    return
                pool.wait_ge(V_rdy, i * 16 + (8 * bb + CR_VR))
                for n in range(4):
                    k, c0, w = PIECES[n][1:]
                    hi, lo, src = cTh[:, 1 - bb, k, c0:c0 + w], cTl[:, 1 - bb, k, c0:c0 + w], raw[:, n % 2, 0:w]
                    pool.wait_ge(raw_in[n % 2], i * (NP_ * 16) + (NP_ * 8 * (bb + 1) + 16 * (n // 2 + 1)))
                    pool.sem_inc(pool_go, 1)
                    pool.tensor_copy(hi, src).then_inc(split_hi, 1)
                    pool.wait_ge(split_hi, i * 8 + (4 * bb + n + 1))
                    pool.tensor_tensor(lo, src, hi.bitcast(F32), ALU.subtract).then_inc(ctxT_rdy, 1)
                    pool.wait_ge(ctxT_rdy, i * 8 + (4 * bb + n + 1 + 4))
                    pool.sem_inc(raw_free, 1)

            with pool.Fori(0, NB // 2 - 1) as i:
                for bb in range(2):
                    split_context(i, bb, False)
            for bb in range(2):
                split_context(NB // 2 - 1, bb, bb == 1)

            def comb_zeros(n):
                pool.wait_ge(ln_stat, 2 * n + 2)
                pool.memset(comb[0:32, :].bitcast(F32), 0.0).then_inc(comb_set, 1)

            if stop == "A":
                return
            comb_zeros(0)
            if stop == "B":
                return

            pool.wait_ge(ln_stat, 3)
            pool.memset(qs[96:97, :, :, :].bitcast(F32), 1.0).then_inc(q_set, 1)

            def split_tile(i, c, u):
                k = u * NPOOL + c // 2
                part = (slice(0, P), c, slice(512, 1024))
                pool.wait_ge(p_clip, i * IT + (u * NCH + c + 1))
                pool.sem_inc(pool_go, 1)
                pool.tensor_copy(ph[part], p32[part]).then_inc(pool_ph, 1)
                pool.wait_ge(pool_ph, i * (2 * NPOOL) + (k + 1))
                pool.tensor_tensor(pl[part], p32[part], ph[part].bitcast(F32), ALU.subtract).then_inc(pool_pl, 1)

            with pool.Fori(0, NJ // 2) as i:
                for u in range(2):
                    for c in range(0, NCH - 1, 2):
                        split_tile(i, c, u)
            if stop == "D":
                comb_zeros(1)

        def mm3(e, o, lh, ll, rh, rl, first, last):
            e.matmul(o, lh, rh, start=first, stop=False, skip_group_check=True)
            e.matmul(o, lh, rl, start=False, stop=False, skip_group_check=True)
            return e.matmul(o, ll, rh, start=False, stop=last, skip_group_check=True)

        @block.tensor
        def _(pe):
            def ln_transpose(n):
                for q in range(4):
                    pe.wait_ge(ln_xn, 8 * n + 2 * q + 2)
                    for k in range(KT):
                        for j in range(2):
                            mm = pe.transpose(ps[:, q, (2 * k + j) * P:(2 * k + j + 1) * P], xn[:, 2 * q + j, k * P:(k + 1) * P], ident[:])
                    mm.then_inc(ln_T, 1)

            pe.wait_ge(cst_in, 16)
            pe.wait_ge(cst_set, 3)
            ln_transpose(0)
            pe.sem_inc(V_rdy, CR_VR)
            pe.sem_inc(R_rdy, 1)
            pe.wait_ge(ln_lo, 4)

            with pe.Fori(0, NB // 2) as pair:
                for bb in range(2):
                    b = pair * 2 + bb
                    for st in range(2):
                        def kproj(n):
                            mt, (c0, w) = n // 4, MCH[n % 4]
                            o = ps[:, 6 + n % 2, 0:w]
                            if n % 4 < 2:
                                pe.wait_ge(V_ev, b * 8 + (4 * (n // 4) + n % 2 - 2 + 1 + VCR))
                            else:
                                pe.wait_ge(K_ev, b * 8 + (n - 2 + 1))
                            for k in range(KT):
                                mm = mm3(pe, o, wkh[:, k, mt * P:(mt + 1) * P], wkl[:, k, mt * P:(mt + 1) * P],
                                         cTh[:, bb, k, c0:c0 + w], cTl[:, bb, k, c0:c0 + w], k == 0, k == KT - 1)
                            mm.then_inc(K_rdy, 1)

                        def vproj(n):
                            m0, cnt = VUNITS[n]
                            if n % 4 < 2:
                                pe.wait_ge(K_ev, b * 8 + (4 * (n // 4) + 2 + n % 2 + 1))
                            else:
                                pe.wait_ge(V_ev, b * 8 + (n - 2 + 1 + VCR))
                            for i in range(cnt):
                                rows = TAIL if m0 + i == MT - 1 else P
                                for k in range(KT):
                                    s = slice((m0 + i) * P, (m0 + i) * P + rows)
                                    mm = mm3(pe, ps[0:rows, 6 + n % 2, i * D:(i + 1) * D], cTh[:, bb, k, s], cTl[:, bb, k, s],
                                             wvh[:, k, :], wvl[:, k, :], k == 0, k == KT - 1)
                            mm.then_inc(V_rdy, 1)
                            return mm

                        def trans(g):
                            if g >= 2:
                                pe.wait_ge(pTl_rdy, b * 8 + (4 * st + g - 2 + 1))
                            for m in range(4 * g, min(4 * g + 4, MT)):
                                rows = TAIL if m == MT - 1 else P
                                mm = pe.transpose(ps[0:rows, 4 + g % 2, (m % 4) * P:(m % 4 + 1) * P], prob[:, m * P:m * P + rows], ident[:])
                            mm.then_inc(T_rdy, 1)

                        if st == 0:
                            pe.wait_ge(xc_rdy, b + 1)
                            pe.wait_ge(neg_rdy, b + 1)
                            pe.wait_ge(ctxT_rdy, b * 4 + 4)
                        for c in (1, 2, 3, 0):
                            c0, w = MCH[c]
                            if c == 0:
                                pe.wait_ge(R_ev, b * 2 + (st + 1))
                            for k in range(KT):
                                mm3(pe, ps[:, c, 0:w], xch[:, k, st * P:(st + 1) * P], xcl[:, k, st * P:(st + 1) * P],
                                    cTh[:, bb, k, c0:c0 + w], cTl[:, bb, k, c0:c0 + w], k == 0, False)
                            mm = pe.matmul(ps[:, c, 0:w], one_row[:], neg[:, c0:c0 + w], start=False, stop=True, skip_group_check=True)
                        mm.then_inc(S_rdy, 1)
                        if st == 0:
                            pe.wait_ge(wkv_rdy, 4)
                        kproj(4 * st)
                        kproj(4 * st + 1)
                        pe.wait_ge(exp_rdy, b * 2 + (st + 1))
                        trans(0)
                        trans(1)
                        kproj(4 * st + 2)
                        kproj(4 * st + 3)
                        trans(2)
                        trans(3)
                        for n in range(4 * st, 4 * st + 4):
                            vproj(n)
                        pe.wait_ge(pTl_rdy, b * 8 + (4 * st + 4))
                        if st == 0:
                            pe.wait_ge(ctxN_rdy, b * 4 + 4)
                        for m in range(MT):
                            rows = TAIL if m == MT - 1 else P
                            mm = mm3(pe, ps[:, 0, 0:D], pTh[0:rows, m, :], pTl[0:rows, m, :], cNh[0:rows, m, :], cNl[0:rows, m, :], m == 0, m == MT - 1)
                        mm.then_inc(R_rdy, 1)
            if stop == "A":
                return

            def ffn(f):
                sh, ex, c0, e0, n = f["sh"], f["ex"], f["c0"], f["e0"], f["n"]
                ln_transpose(f["ln"])
                pe.wait_ge(ln_lo, 4 * f["ln"] + 4)
                pe.wait_ge(gw_rdy, n + 1)
                for half in range(2):
                    for k in range(KT):
                        s = slice(half * 512, half * 512 + 512)
                        mm = mm3(pe, ps[0:E, 6 + half, :], gwh[:, k, :], gwl[:, k, :], xTh[:, k, s], xTl[:, k, s], k == 0, k == KT - 1)
                mm.then_inc(LT_rdy, 1)
                for n_ in range(4 * 4):
                    mm = pe.matmul(psf[:, n_ * P:(n_ + 1) * P], zero[:], zero[:], start=True, stop=False, skip_group_check=True)

                def logits_T():
                    pe.wait_ge(LT_ev, n + 1)
                    for t in range(NT):
                        mm = pe.transpose(ps[:, 7, t * E:(t + 1) * E], logit[:, t * P:(t + 1) * P], ident[0:E, 0:E])
                    mm.then_inc(L_rdy, 1)

                def weights_T():
                    pe.wait_ge(g_chain, GC[n][-1])
                    for t in range(NT):
                        mm = pe.transpose(ps[0:E, 6 + t // 4, (t % 4) * P:(t % 4 + 1) * P], g_w[:, t, :], ident[:])
                    mm.then_inc(gT_rdy, 1)

                def hidden(ct, tiles, slot, half, exp, first, ec):
                    s = slice(half * 512, half * 512 + 512)
                    if half == 0:
                        pe.wait_ge(w_rdy, tiles)
                    if not first:
                        pe.wait_ge(silu_rdy, ct)
                    for k in range(KT):
                        mm = mm3(pe, ps[:, 4, :], w_hi[:, slot, k * P:(k + 1) * P], w_lo[:, slot, k * P:(k + 1) * P], xTh[:, k, s], xTl[:, k, s], k == 0, k == 1)
                    mm.then_inc(G_rdy, 1)
                    if isinstance(ct, int) and ct == c0:
                        logits_T()
                    if not first:
                        pe.wait_ge(mul1_rdy, ct)
                    for k in range(KT):
                        w = slice(D + k * P, D + (k + 1) * P)
                        mm = mm3(pe, ps[:, 5, :], w_hi[:, slot, w], w_lo[:, slot, w], xTh[:, k, s], xTl[:, k, s], k == 0, k == 1)
                    mm.then_inc(U_rdy, 1)
                    if exp:
                        if ec is not None:
                            pe.wait_ge(mul2_rdy, ec)
                        pe.matmul(ps[:, 6, :], w_hi[0:CROWS, slot, 3 * D:WC], comb[:, s], start=True, stop=True).then_inc(C_rdy, 1)

                def down(ct, slot, half):
                    pe.wait_ge(hl_rdy, ct + 1)
                    buf = half
                    for j in range(4):
                        t = 4 * half + j
                        s = slice(j * P, (j + 1) * P)
                        mm = mm3(pe, ps[:, t // 2, (t % 2) * D:(t % 2 + 1) * D], hh[:, buf, s], hl[:, buf, s],
                                 w_hi[:, slot, 2 * D:3 * D], w_lo[:, slot, 2 * D:3 * D], False, False)
                    mm.then_inc(down_done, 1)

                prev = None
                for k in range(sh):
                    for half in range(2):
                        ct = c0 + 2 * k + half
                        slot = (f["t0"] + k) % 2
                        hidden(ct, f["t0"] + k + 1, slot, half, False, k == 0 and half == 0 and n == 0, None)
                        if k == sh - 1 and half == 1:
                            weights_T()
                        if prev:
                            down(*prev)
                        prev = (ct, slot, half)
                pe.wait_ge(combl_rdy, n + 1)
                tb = f["t0"] + sh

                def step(i, j, half, first):
                    ct = i * 4 + (2 * tb + 2 * j + half)
                    slot = (tb + j) % 2
                    ec = None if (first and n == 0) else i * 4 + (e0 + 2 * j + half)
                    hidden(ct, i * 2 + (tb + j + 1), slot, half, True, False, ec)
                    pct = i * 4 + (2 * tb + 2 * j + half - 1)
                    down(pct, slot if half else (tb + j - 1) % 2, (half + 1) % 2)

                for j in range(2):
                    for half in range(2):
                        step(0, j, half, j == 0 and half == 0)
                with pe.Fori(1, ex // 2) as i:
                    for j in range(2):
                        for half in range(2):
                            step(i, j, half, False)
                last = 2 * (tb + ex) - 1
                down(last, (tb + ex - 1) % 2, 1)

            ffn(FFN["B"])
            if stop == "B":
                return

            pe.sem_inc(sc_rdy, CR_SC)
            pe.sem_inc(pv_done, CR_PV)
            ln_transpose(2)
            pe.wait_ge(ln_lo, 12)
            pe.wait_ge(cw_rdy, 4)
            for n in range(2 * NPAIR):
                t, half = n // 2, n % 2
                s = slice(half * 512, half * 512 + 512)
                if n >= 4:
                    pe.wait_ge(q_32, n - 4 + 1)
                for k in range(KT):
                    mm = mm3(pe, ps[0:3 * PR, 4 + n % 4, :], wqh[:, k, t, :], wql[:, k, t, :], xTh[:, k, s], xTl[:, k, s], k == 0, k == 1)
                mm.then_inc(Q_rdy, 1)
            pe.wait_ge(q_lo, 4 * NPAIR)
            pe.wait_ge(q_set, 1)

            def qk(i, y):
                u, c = at(y)
                if c == 0:
                    pe.wait_ge(kv_in[u % 2], i * 80 + (80 * (u // 2) + 80))
                bank = 2 * (y % 2)
                pe.wait_ge(p_exp, i * IT + (y + 1))
                for m in range(2 * c, min(2 * c + 2, MT)):
                    rows = TAIL if m == MT - 1 else P
                    mm = pe.matmul(ps[0:rows, bank + m % 2, :], kslot[0:QROWS, u % 2, m * P:m * P + rows],
                                   qs[0:QROWS, bass.ds(i * 2 + u, 1), :, :].rearrange("p o h s -> p (o h s)"), start=True, stop=True)
                mm.then_inc(sc_rdy, 1)

            def pv(i, y):
                u, c = at(y)
                if c == 0:
                    pe.wait_ge(oT_rdy, i * 2 + (u + 1))
                pe.wait_ge(pl_rdy, i * IT + (y + 1))
                if c % 2 == 0 and c < NCH - 1:
                    pe.wait_ge(pool_pl, i * (2 * NPOOL) + (u * NPOOL + c // 2 + 1))
                for m in range(2 * c, min(2 * c + 2, MT)):
                    rows = TAIL if m == MT - 1 else P
                    v = vslot[0:rows, u % 2, m * VC:(m + 1) * VC]
                    s = slice((m % 2) * 512, (m % 2) * 512 + 512)
                    if c in NATIVE and m % 2:
                        mm = pe.matmul(ps[0:VC, 4 + u % 2, :], v.bitcast(F32), p32[0:rows, c, s], start=False, stop=False, skip_group_check=True)
                        continue
                    pe.matmul(ps[0:VC, 4 + u % 2, :], v, ph[0:rows, c, s], start=(m == 0), stop=False, skip_group_check=True)
                    mm = pe.matmul(ps[0:VC, 4 + u % 2, :], v, pl[0:rows, c, s], start=False, stop=(m == MT - 1), skip_group_check=True)
                mm.then_inc(pv_done, 1)

            def osum(i, u):
                pe.wait_ge(oT_rdy, i * 2 + (u + 1 + 2))
                pe.wait_ge(cx_rdy, i * 2 + (u + 1))
                for h in range(2):
                    for st in range(2):
                        mm = pe.matmul(ps[:, 6, (2 * h + st) * 32:(2 * h + st) * 32 + HD + 1],
                                       oT[:, u % 2, h * SEQ + st * P:h * SEQ + (st + 1) * P], msum[:, h, :], start=True, stop=True)
                mm.then_inc(osum_rdy, 1)

            def step(i, x):
                if alive(i, x + 2, IT):
                    qk(i, x + 2)
                if (x - OSUM_LAG) % NCH == 0 and alive(i, (x - OSUM_LAG) // NCH, 2):
                    osum(i, (x - OSUM_LAG) // NCH)
                if alive(i, x - PV_LAG, IT):
                    pv(i, x - PV_LAG)

            qk(0, 0)
            qk(0, 1)
            for x in range(IT):
                step(0, x)
            with pe.Fori(1, NJ // 2 - 1) as i:
                for x in range(IT):
                    step(i, x)
            for x in range(DRAIN):
                step(NJ // 2 - 1, x)

            pe.wait_ge(cx_rdy, NJ + 1)
            for q in range(4):
                for k in range(KT):
                    for j in range(2):
                        src = cx[:, j, q * NPAIR + 4 * k:q * NPAIR + 4 * k + 4, :].rearrange("p t r -> p (t r)")
                        mm = pe.transpose(ps[:, q, (2 * k + j) * P:(2 * k + j + 1) * P], src, ident[:])
                mm.then_inc(cT_rdy, 1)
            for q in range(4):
                pe.wait_ge(cTl_rdy, q + 1)
                for j in range(2):
                    for k in range(KT):
                        s = slice((2 * k + j) * P, (2 * k + j + 1) * P)
                        mm = mm3(pe, ps[:, 4 + q, j * D:(j + 1) * D], cTxh[:, q, s], cTxl[:, q, s], woh[:, k, :], wol[:, k, :], k == 0, k == 1)
                mm.then_inc(dl_rdy, 1)
            if stop == "C":
                return
            ffn(FFN["D"])

        @block.scalar
        def _(act):
            def ln_std_hi(n):
                act.wait_ge(ln_mv, 8 * n + 8)
                act.activation(std[:], mv[:, :, 1], ACT.Sqrt, bias=eps[:]).then_inc(ln_std, 1)
                for q in range(4):
                    act.wait_ge(ln_T, 4 * n + q + 1)
                    act.activation(xTh[:, :, q * 256:(q + 1) * 256], ps[:, q, :].rearrange("p (k n) -> p k n", k=KT), ACT.Copy).then_inc(ln_hi, 1)

            act.wait_ge(cst_set, 3)
            ln_std_hi(0)
            for n in range(4):
                k, c0, w = PIECES[n][1:]
                act.wait_ge(raw_in[n % 2], 16 * (n // 2 + 1))
                act.activation(cTh[:, 0, k, c0:c0 + w], raw[:, n % 2, 0:w], ACT.Copy).then_inc(first_hi, 1)
            act.wait_ge(vstk_set, 2)
            act.sem_inc(v_out, 16)
            for n in range(2):
                act.sem_inc(k_out[n], 32)
            with act.Fori(0, NB) as b:
                for st in range(2):
                    def kev(n):
                        mt, (c0, w) = n // 4, MCH[n % 4]
                        act.wait_ge(K_rdy, b * 8 + (n + 1))
                        act.wait_ge(k32_free, b * 8 + (n + 1))
                        act.wait_ge(k_out[n % 2], b * 128 + (32 * (n // 2) + 32))
                        act.activation(k32[:, n % 2, 0:w], ps[:, 6 + n % 2, 0:w], ACT.Identity, bias=bk[:, mt:mt + 1]).then_inc(k32_rdy, 1)
                        act.activation(kh[:, n % 2, 0:w], ps[:, 6 + n % 2, 0:w], ACT.Identity, bias=bk[:, mt:mt + 1]).then_inc(K_ev, 1)

                    def nat_hi(n):
                        c0, w = PIECES[4 + n][2:]
                        act.wait_ge(R_rdy, b * 2 + 1)
                        act.wait_ge(raw_in[n % 2], b * (8 * NP_) + 16 * (2 + n // 2 + 1))
                        act.activation(cNh[:, c0:c0 + w, :], raw[:, n % 2, 0:w * D].rearrange("p (t d) -> p t d", d=D), ACT.Copy).then_inc(ctxN_hi, 1)

                    def pth(g):
                        act.wait_ge(T_rdy, b * 8 + (4 * st + g + 1))
                        if g < 3:
                            act.activation(pTh[:, 4 * g:4 * g + 4, :], ps[:, 4 + g % 2, :].rearrange("p (m s) -> p m s", s=P), ACT.Copy).then_inc(pTh_rdy, 1)
                        else:
                            act.activation(pTh[0:TAIL, MT - 1, :], ps[0:TAIL, 5, 0:P], ACT.Copy).then_inc(pTh_rdy, 1)

                    kev(4 * st)
                    act.wait_ge(nmax_rdy, b * 2 + (st + 1))
                    act.activation(prob[:, 0:MP], psf[:, 0:MP], ACT.Exp, scale=1.0 / 16, bias=nmax[:], accum_out=psum_[:]).then_inc(exp_rdy, 1)
                    if st == 0:
                        nat_hi(0)
                        nat_hi(1)
                    kev(4 * st + 1)
                    act.wait_ge(R_rdy, b * 2 + (st + 1))
                    pth(0)
                    pth(1)
                    kev(4 * st + 2)
                    if st == 0:
                        nat_hi(2)
                        nat_hi(3)
                    kev(4 * st + 3)
                    pth(2)
                    pth(3)
                    for n in range(4 * st, 4 * st + 4):
                        m0, cnt = VUNITS[n]
                        rows = TAIL if m0 == MT - 1 else P
                        if n == 0:
                            act.wait_ge(v_out, b * 16 + 16)
                        act.wait_ge(V_ev, b * 8 + (n + 1 + VCR))
                        for i in range(cnt):
                            h = act.activation(vstk[0:rows, :, m0 + i, 0:PR], v32[0:rows, n % 2, i, :].rearrange("p (t r) -> p t r", r=PR), ACT.Copy)
                        h.then_inc(vh_rdy, 1)
            if stop == "A":
                return

            def ffn(f):
                n, c0, sh, ex = f["n"], f["c0"], f["sh"], f["ex"]
                ln_std_hi(f["ln"])
                act.wait_ge(LT_rdy, n + 1)
                act.activation(logit[:].rearrange("e (b s) -> e b s", b=2), ps[0:E, 6:8, :], ACT.Copy).then_inc(LT_ev, 1)
                act.wait_ge(L_rdy, n + 1)
                lg = ps[:, 7, 0:NT * E]
                if n == 0:
                    act.activation(g_s[:].rearrange("p t e -> p (t e)"), lg, ACT.Sigmoid).then_inc(g_act, 1)
                else:
                    act.wait_ge(g_chain, GC[1][1])
                    act.activation(g_s[:].rearrange("p t e -> p (t e)"), g_c[:].rearrange("p t e -> p (t e)"), ACT.Exp).then_inc(g_act, 1)
                def chunk(ct, half, mulsem, mulval, wait_hh=True):
                    act.wait_ge(G_rdy, ct + 1)
                    act.activation(silu[:, half, :], ps[:, 4, :], ACT.Silu).then_inc(silu_rdy, 1)
                    act.wait_ge(mulsem, mulval)
                    if wait_hh:
                        act.wait_ge(down_done, ct - 1)
                    act.activation(hh[:, half, :], h32[:, half, :], ACT.Copy).then_inc(hh_rdy, 1)

                for k in range(sh):
                    for half in range(2):
                        ct = c0 + 2 * k + half
                        chunk(ct, half, mul1_rdy, ct + 1, ct >= 2)
                act.wait_ge(gT_rdy, n + 1)
                act.wait_ge(comb_set, n + 1)
                act.activation(comb[0:E, :].rearrange("e (b s) -> e b s", b=2), ps[0:E, 6:8, :], ACT.Copy).then_inc(combh_rdy, 1)
                with act.Fori(0, ex // 2) as i:
                    for j in range(4):
                        ct = i * 4 + (c0 + 2 * sh + j)
                        chunk(ct, j % 2, mul2_rdy, i * 4 + (f["e0"] + j + 1))

            ffn(FFN["B"])
            if stop == "B":
                return

            ln_std_hi(2)
            act.wait_ge(bq_rdy, 1)
            for n in range(2 * NPAIR):
                t, half = n // 2, n % 2
                act.wait_ge(Q_rdy, n + 1)
                if n >= 4:
                    act.wait_ge(q_lo, 2 * (n - 4) + 2)
                act.activation(q32[0:3 * PR, n % 4, :], ps[0:3 * PR, 4 + n % 4, :], ACT.Identity, bias=bq[0:3 * PR, t:t + 1]).then_inc(q_32, 1)
                dst, src = q_parts(n, 1)
                act.wait_ge(q_32, n + 1)
                act.activation(dst, src, ACT.Identity, scale=hmask[0:3 * PR, 1:2], bias=zero[0:3 * PR, 0:1].bitcast(F32)).then_inc(q_hi, 1)
            act.sem_inc(p_exp, 2)
            act.sem_inc(oT_rdy, 2)

            def exp_chunk(i, y):
                u, c = at(y)
                bank = 2 * (y % 2)
                act.wait_ge(sc_rdy, i * IT + (y + 1 + CR_SC))
                act.wait_ge(pv_done, i * IT + (y - NCH + 1 + CR_PV))
                rows, w = (P, 1024) if c < NCH - 1 else (TAIL, 512)
                act.activation(p32[0:rows, c, 0:w], psf[0:rows, bank * 512:bank * 512 + w], ACT.Exp, scale=0.25).then_inc(p_exp, 1)

            def hi_chunk(i, y):
                u, c = at(y)
                act.wait_ge(p_clip, i * IT + (y + 1))
                rows, w = split_part(c)
                act.activation(ph[0:rows, c, 0:w], p32[0:rows, c, 0:w], ACT.Copy).then_inc(ph_rdy, 1)

            def step(i, x):
                if alive(i, x, IT):
                    exp_chunk(i, x)
                y = x - HI_LAG
                if alive(i, y, IT):
                    hi_chunk(i, y)

            for x in range(IT):
                step(0, x)
            with act.Fori(1, NJ // 2 - 1) as i:
                for x in range(IT):
                    step(i, x)
            for x in range(DRAIN):
                step(NJ // 2 - 1, x)
            for q in range(4):
                act.wait_ge(cT_rdy, q + 1)
                act.activation(cTxh[:, q, :], ps[:, q, :], ACT.Copy).then_inc(cTh_rdy, 1)
            act.wait_ge(dl_a, DLA)
            act.activation(std[:], mv[:, :, 1], ACT.Sqrt, bias=eps[:]).then_inc(dl_std, 1)
            if stop == "C":
                return
            ffn(FFN["D"])

        @block.vector
        def _(dve):
            def ln_front(n):
                for t in range(NT):
                    s = dve.bn_stats(st6[:, t, :], resid[:, t, :])
                s.then_inc(ln_stat, 1)
                dve.wait_ge(ln_stat, n + 1)
                for t in range(NT):
                    dve.bn_aggr(mv[:, t, :], st6[:, t, :]).then_inc(ln_mv, 1)
                dve.wait_ge(ln_std, n + 1)
                dve.reciprocal(rstd[:], std[:]).then_inc(ln_rstd, 1)
                dve.wait_ge(ln_rstd, n + 1)
                for t in range(NT):
                    dve.tensor_scalar(xn[:, t, :], resid[:, t, :], mv[:, t, 0:1], rstd[:, t:t + 1], ALU.subtract, ALU.mult).then_inc(ln_xn, 1)

            def ln_back(n):
                for q in range(4):
                    dve.wait_ge(ln_hi, 4 * n + q + 1)
                    s = slice(q * 256, (q + 1) * 256)
                    dve.tensor_tensor(xTl[:, :, s], ps[:, q, :].rearrange("p (k n) -> p k n", k=KT), xTh[:, :, s].bitcast(F32), ALU.subtract).then_inc(ln_lo, 1)

            def rank_compare(link, v, tri, w, part=None):
                eq = g_eq[:].rearrange("p a b -> p (a b)")[:, 0:NT * w * w]
                big = g_big[:].rearrange("p a b -> p (a b)")[:, 0:NT * w * w]
                vj = v.unsqueeze(2).broadcast_to([P, NT, w, w])
                ve = v.unsqueeze(3).broadcast_to([P, NT, w, w])
                if part != 2:
                    dve.tensor_tensor(big.rearrange("p (t e j) -> p t e j", e=w, j=w), vj, ve, ALU.is_gt)
                    link(dve.tensor_tensor(eq.rearrange("p (t e j) -> p t e j", e=w, j=w), vj, ve, ALU.is_equal))
                if part != 1:
                    eq3 = eq.rearrange("p (t n) -> p t n", n=w * w)
                    link(dve.tensor_tensor(eq3, eq3, tri[:].unsqueeze(1).broadcast_to([P, NT, w * w]), ALU.mult))
                    link(dve.tensor_tensor(big, big, eq, ALU.add))

            def rank_count(link, out_, w):
                big = g_big[:].rearrange("p a b -> p (a b)")[:, 0:NT * w * w]
                link(dve.tensor_reduce(out_, big.rearrange("p (a j) -> p a j", j=w), AX.X, ALU.add))

            dve.wait_ge(x_in, 16)
            ln_front(0)
            ln_back(0)
            dve.sem_inc(att_free, 1)
            dve.sem_inc(k32_free, 2)
            dve.sem_inc(V_ev, VCR)
            dve.sem_inc(R_ev, 1)
            dve.sem_inc(rs_chain, 1)
            dve.wait_ge(ln_lo, 4)
            def masks(b):
                dve.tensor_copy(xch[:], xTh[:, :, bass.ds(b * SEQ, SEQ)].bitcast(F32))
                dve.tensor_copy(xcl[:], xTl[:, :, bass.ds(b * SEQ, SEQ)].bitcast(F32)).then_inc(xc_rdy, 1)
                dve.wait_ge(att_in, b * 16 + 16)
                dve.tensor_scalar(neg[:], attend[0:1, :], 1.0, 1.6e31, ALU.subtract, ALU.mult).then_inc(neg_rdy, 1)
                dve.tensor_reduce(valid[:], attend, AX.X, ALU.max).then_inc(valid_rdy, 1)
                dve.wait_ge(valid_rdy, b + 1)
                dve.sem_inc(att_free, 1)
                dve.wait_ge(mi_in, b * 16 + 16)
                dve.tensor_scalar(mneg, mi[:], 0.5, -4e30, ALU.is_le, ALU.mult).then_inc(mneg_rdy, 1)

            def batch(b, last):
                for st in range(2):
                    def klo(n):
                        w = MCH[n % 4][1]
                        dve.wait_ge(K_ev, b * 8 + (n + 1))
                        dve.tensor_tensor(kl[:, n % 2, 0:w], k32[:, n % 2, 0:w], kh[:, n % 2, 0:w].bitcast(F32), ALU.subtract).then_inc(kl_rdy, 1)
                        dve.wait_ge(kl_rdy, b * 8 + (n + 1))
                        dve.sem_inc(k32_free, 1)

                    def ptl(g):
                        dve.wait_ge(pTh_rdy, b * 8 + (4 * st + g + 1))
                        if g < 3:
                            dve.tensor_tensor(pTl[:, 4 * g:4 * g + 4, :], ps[:, 4 + g % 2, :].rearrange("p (m s) -> p m s", s=P),
                                              pTh[:, 4 * g:4 * g + 4, :].bitcast(F32), ALU.subtract).then_inc(pTl_rdy, 1)
                        else:
                            dve.tensor_tensor(pTl[0:TAIL, MT - 1, :], ps[0:TAIL, 5, 0:P], pTh[0:TAIL, MT - 1, :].bitcast(F32), ALU.subtract).then_inc(pTl_rdy, 1)

                    dve.wait_ge(S_rdy, b * 2 + (st + 1))
                    dve.tensor_reduce(rmax[:], psf[:, 0:MP], AX.X, ALU.max).then_inc(max_rdy, 1)
                    dve.wait_ge(max_rdy, b * 2 + (st + 1))
                    dve.tensor_scalar(nmax[:], rmax[:], -1.0 / 16, None, ALU.mult).then_inc(nmax_rdy, 1)
                    klo(4 * st)
                    dve.wait_ge(exp_rdy, b * 2 + (st + 1))
                    dve.reciprocal(rsum[:], psum_[:]).then_inc(rsum_rdy, 1)
                    klo(4 * st + 1)
                    dve.wait_ge(rsum_rdy, b * 2 + (st + 1))
                    dve.tensor_tensor(rscale[:], rsum[:], valid[:], ALU.mult).then_inc(rscale_rdy, 1)
                    ptl(0)
                    ptl(1)
                    klo(4 * st + 2)
                    klo(4 * st + 3)
                    ptl(2)
                    ptl(3)

                    def vpart(n):
                        m0, cnt = VUNITS[n]
                        rows = TAIL if m0 == MT - 1 else P
                        return rows, m0, cnt

                    for n in range(4 * st, 4 * st + 4):
                        rows, m0, cnt = vpart(n)
                        dve.wait_ge(V_rdy, b * 8 + (n + 1 + CR_VR))
                        dve.tensor_tensor(v32[0:rows, n % 2, 0:cnt, :], ps[0:rows, 6 + n % 2, 0:cnt * D].rearrange("p (i d) -> p i d", d=D),
                                          bv[0:rows, :].unsqueeze(1).broadcast_to([rows, cnt, D]), ALU.add).then_inc(V_ev, 1)
                        dve.wait_ge(vh_rdy, b * 8 + (n + 1))
                        for i in range(cnt):
                            l = dve.tensor_tensor(vstk[0:rows, :, m0 + i, PR:2 * PR], v32[0:rows, n % 2, i, :].rearrange("p (t r) -> p t r", r=PR),
                                                  vstk[0:rows, :, m0 + i, 0:PR].bitcast(F32), ALU.subtract)
                        l.then_inc(vl_rdy, 1)
                    if st == 1 and not last:
                        masks(b + 1)
                    dve.wait_ge(R_rdy, b * 2 + (st + 2))
                    dve.wait_ge(rscale_rdy, b * 2 + (st + 1))
                    x = resid[:, bass.ds(b * 2 + st, 1), :].rearrange("p o d -> p (o d)")
                    dve.scalar_tensor_tensor(out=x, in0=ps[:, 0, 0:D], scalar=rscale[:], in1=x, op0=ALU.mult, op1=ALU.add).then_inc(R_ev, 1)

            def first_lo(n):
                k, c0, w = PIECES[n][1:]
                dve.wait_ge(first_hi, n + 1)
                dve.tensor_tensor(cTl[:, 0, k, c0:c0 + w], raw[:, n % 2, 0:w], cTh[:, 0, k, c0:c0 + w].bitcast(F32), ALU.subtract).then_inc(ctxT_rdy, 1)
                dve.wait_ge(ctxT_rdy, n + 1)
                dve.sem_inc(raw_free, 1)

            first_lo(0)
            first_lo(1)
            masks(0)
            first_lo(2)
            first_lo(3)
            dve.wait_ge(wkv_in, 64)
            for raw_, h, l in ((wk_raw, wkh, wkl), (wv_raw, wvh, wvl)):
                dve.tensor_copy(h[:], raw_[:]).then_inc(wkv_hi, 1)
            dve.wait_ge(wkv_hi, 2)
            for raw_, h, l in ((wk_raw, wkh, wkl), (wv_raw, wvh, wvl)):
                dve.tensor_tensor(l[:], raw_[:], h[:].bitcast(F32), ALU.subtract).then_inc(wkv_rdy, 2)
            dve.wait_ge(wkv_rdy, 4)
            with dve.Fori(0, NB - 1) as b:
                batch(b, False)
            batch(NB - 1, True)
            dve.wait_ge(R_ev, 2 * NB + 1)
            if stop == "A":
                dve.sem_inc(out_go, 1)
                return

            def attention_weights_hi():
                dve.wait_ge(cw_in, 16 * 16)
                for r, h in ((wq_raw[:], wqh[:]), (wo_raw[:], woh[:])):
                    dve.tensor_copy(h, r).then_inc(cwh, 1)

            def attention_weights_lo():
                dve.wait_ge(cwh, 2)
                flat = lambda t: t.rearrange("p k t n -> p (k t n)")
                dve.tensor_tensor(flat(wql[:]), flat(wq_raw[:]), flat(wqh[:]).bitcast(F32), ALU.subtract).then_inc(cw_rdy, 2)
                dve.tensor_tensor(wol[:], wo_raw[:], woh[:].bitcast(F32), ALU.subtract).then_inc(cw_rdy, 2)
                dve.tensor_scalar(rs[:], rs[:], 0.0, 0.3, ALU.max, ALU.min).then_inc(bq_rdy, 1)
                dve.wait_ge(bq_rdy, 1)
                dve.tensor_scalar(bo[:], bo[:], rs[:], None, ALU.mult).then_inc(bq_rdy, 1)
                dve.wait_ge(bq_rdy, 2)

            def ffn(f):
                n, c0, sh, ex, e0 = f["n"], f["c0"], f["sh"], f["ex"], f["e0"]
                t0 = f["t0"]

                def split(tn, slot, cnt, down=None):
                    dve.wait_ge(w_in[slot], cnt)
                    if down is not None:
                        dve.wait_ge(down_done, down)
                    dve.tensor_copy(w_hi[:, slot, :], w_raw[:, slot, :]).then_inc(w_hi_rdy, 1)
                    dve.wait_ge(w_hi_rdy, tn)
                    dve.tensor_tensor(w_lo[:, slot, :], w_raw[:, slot, 0:3 * D], w_hi[:, slot, 0:3 * D].bitcast(F32), ALU.subtract).then_inc(w_rdy, 1)
                    dve.wait_ge(w_rdy, tn)
                    dve.sem_inc(wraw_free, 1)

                ln_front(f["ln"])
                dve.wait_ge(gate_in, 64 * (n + 1))
                dve.tensor_copy(gwh[:], gw_raw[:]).then_inc(gwh_rdy, 1)
                dve.wait_ge(gwh_rdy, n + 1)
                dve.tensor_tensor(gwl[:], gw_raw[:], gwh[:].bitcast(F32), ALU.subtract).then_inc(gw_rdy, 1)
                ln_back(f["ln"])
                split(t0 + 1, t0 % 2, 16 * (t0 // 2 + 1))
                split(t0 + 2, (t0 + 1) % 2, 16 * ((t0 + 1) // 2 + 1))

                seen = [GC[n][0]]

                def link(ins):
                    seen[0] += 1
                    ins.then_inc(g_chain, 1)
                    dve.wait_ge(g_chain, seen[0])

                bias = gb[:].unsqueeze(1).broadcast_to([P, NT, E])
                top, scale = (6.0, 2.5) if n == 0 else (2.0, None)
                lg = ps[:, 7, 0:NT * E].rearrange("p (t e) -> p t e", e=E)

                def shifted():
                    dve.wait_ge(L_rdy, 2)
                    link(dve.tensor_reduce(g_t[:], lg, AX.X, ALU.max))
                    link(dve.tensor_tensor(g_c[:], lg, g_t[:].unsqueeze(2).broadcast_to([P, NT, E]), ALU.subtract))
                    assert seen[0] == GC[1][1]

                def choice():
                    dve.wait_ge(g_act, n + 1)
                    if n == 0:
                        link(dve.tensor_tensor(g_c[:], g_s[:], bias, ALU.add))
                        v = g_c[:].rearrange("p t (g e) -> p (t g) e", e=4)
                        dve.tensor_tensor(g_pair[:, :, 0:3], v[:, :, 0:3], v[:, :, 1:4], ALU.add)
                        dve.tensor_tensor(g_pair[:, :, 3:5], v[:, :, 0:2], v[:, :, 2:4], ALU.add)
                        link(dve.tensor_tensor(g_pair[:, :, 5:6], v[:, :, 0:1], v[:, :, 3:4], ALU.add))
                        link(dve.tensor_reduce(g_gs[:], g_pair[:], AX.X, ALU.max))
                        gs = g_gs[:].rearrange("p (t g) -> p t g", g=4)
                        rank_compare(link, gs, tri4, 4)
                        rank_count(link, g_gr[:], 4)
                        link(dve.tensor_scalar(g_gr[:], g_gr[:], 2.0, None, ALU.is_lt))
                        link(dve.tensor_tensor(g_c[:].rearrange("p t (g e) -> p (t g) e", e=4), v, g_gr[:].unsqueeze(2).broadcast_to([P, NT * 4, 4]), ALU.mult))
                    else:
                        link(dve.tensor_reduce(g_t[:], g_s[:], AX.X, ALU.add))
                        link(dve.reciprocal(g_r[:], g_t[:]))
                        link(dve.tensor_tensor(g_s[:], g_s[:], g_r[:].unsqueeze(2).broadcast_to([P, NT, E]), ALU.mult))
                        link(dve.tensor_tensor(g_c[:], lg, bias, ALU.add))

                def combine():
                    link(dve.tensor_scalar(g_rank[:], g_rank[:], top, None, ALU.is_lt))
                    link(dve.tensor_tensor(g_w[:], g_rank[:], g_s[:], ALU.mult))
                    link(dve.tensor_reduce(g_t[:], g_w[:], AX.X, ALU.add))
                    if n == 0:
                        link(dve.tensor_scalar(g_t[:], g_t[:], 1e-20, None, ALU.add))
                    link(dve.reciprocal(g_r[:], g_t[:]))
                    link(dve.tensor_tensor(g_w[:], g_w[:], g_r[:].unsqueeze(2).broadcast_to([P, NT, E]), ALU.mult))
                    if n == 0:
                        link(dve.tensor_scalar(g_w[:], g_w[:], scale, None, ALU.mult))
                    assert seen[0] == GC[n][-1], (n, seen[0])

                def chunk(ct, half, exp, ec):
                    dve.wait_ge(silu_rdy, ct + 1)
                    dve.wait_ge(U_rdy, ct + 1)
                    dve.tensor_tensor(h32[:, half, :], silu[:, half, :], ps[:, 5, :], ALU.mult).then_inc(mul1_rdy, 1)
                    if exp:
                        dve.wait_ge(mul1_rdy, ct + 1)
                        dve.wait_ge(C_rdy, ec)
                        dve.tensor_tensor(h32[:, half, :], h32[:, half, :], ps[:, 6, :], ALU.mult).then_inc(mul2_rdy, 1)
                    dve.wait_ge(hh_rdy, ct + 1)
                    dve.tensor_tensor(hl[:, half, :], h32[:, half, :], hh[:, half, :].bitcast(F32), ALU.subtract).then_inc(hl_rdy, 1)

                if n == 1:
                    shifted()
                for k in range(sh):
                    for half in range(2):
                        chunk(c0 + 2 * k + half, half, False, None)
                        step = 2 * k + half
                        if k >= 1 and half == 0:
                            tn = t0 + k + 1
                            split(tn + 1, tn % 2, 16 * (tn // 2 + 1), 2 * tn - 2)
                        first = 1 - n
                        if step == 0:
                            choice()
                        if step == first:
                            rank_compare(link, g_c[:], tri16, E, 1)
                        elif step == first + 1:
                            rank_compare(link, g_c[:], tri16, E, 2)
                        elif step == first + 2:
                            rank_count(link, g_rank[:].rearrange("p t e -> p (t e)"), E)
                            combine()
                dve.wait_ge(combh_rdy, n + 1)
                dve.tensor_tensor(comb[32:CROWS, :].rearrange("e (b s) -> e b s", b=2), ps[0:E, 6:8, :],
                                  comb[0:E, :].bitcast(F32).rearrange("e (b s) -> e b s", b=2), ALU.subtract).then_inc(combl_rdy, 1)

                tb = t0 + sh
                def pair(i, last):
                    for j in range(2):
                        for half in range(2):
                            chunk(i * 4 + (c0 + 2 * sh + 2 * j + half), half, True, i * 4 + (e0 + 2 * j + half + 1))
                            if half == 0 and not (last and j == 1):
                                tn = tb + j + 1
                                split(i * 2 + (tn + 1), tn % 2, i * 16 + 16 * (tn // 2 + 1), i * 4 + (2 * tn - 2))
                if n == 0:
                    attention_weights_hi()
                with dve.Fori(0, ex // 2 - 1) as i:
                    pair(i, False)
                if n == 0:
                    attention_weights_lo()
                pair(ex // 2 - 1, True)
                dve.wait_ge(down_done, 2 * (t0 + sh + ex))
                for q in range(4):
                    x = resid[:, 2 * q:2 * q + 2, :].rearrange("p t d -> p (t d)")
                    dve.tensor_tensor(x, x, ps[:, q, :], ALU.add).then_inc(add_rdy, 1)
                dve.wait_ge(add_rdy, 4 * (n + 1))

            dve.sem_inc(wraw_free, 2)
            ffn(FFN["B"])
            if stop == "B":
                dve.sem_inc(out_go, 1)
                return

            ln_front(2)
            ln_back(2)
            for n in range(2 * NPAIR):
                t, half = n // 2, n % 2
                dve.wait_ge(q_32, n + 1)
                dst, src = q_parts(n, 0)
                dve.tensor_scalar(dst, src, hmask[0:3 * PR, 0:1], None, ALU.mult).then_inc(q_hi0, 1)
                for h in range(2):
                    dst, src = q_parts(n, h)
                    lo = dst[2 * PR:3 * PR]
                    dve.wait_ge((q_hi0, q_hi)[h], n + 1)
                    dve.scalar_tensor_tensor(out=lo, in0=src[2 * PR:3 * PR], scalar=hmask[2 * PR:3 * PR, h:h + 1], in1=lo.bitcast(F32),
                                             op0=ALU.mult, op1=ALU.subtract).then_inc(q_lo, 1)

            dve.sem_inc(cx_rdy, 1)

            def clip(i, y):
                u, c = at(y)
                rows, w = (P, 1024) if c < NCH - 1 else (TAIL, 512)
                t = p32[0:rows, c, 0:w]
                dve.wait_ge(p_exp, i * IT + (y + 1 + 2))
                dve.tensor_scalar(t, t, CLO, CHI, ALU.max, ALU.min).then_inc(p_clip, 1)

            def low(i, y):
                u, c = at(y)
                rows, w = split_part(c)
                dve.wait_ge(ph_rdy, i * IT + (y + 1))
                dve.tensor_tensor(pl[0:rows, c, 0:w], p32[0:rows, c, 0:w], ph[0:rows, c, 0:w].bitcast(F32), ALU.subtract).then_inc(pl_rdy, 1)

            def evac(i, u):
                dve.wait_ge(pv_done, i * IT + (u * NCH + NCH + CR_PV))
                dve.tensor_copy(oT[:, u % 2, :], ps[0:VC, 4 + u % 2, :]).then_inc(oT_rdy, 1)

            def norm(i, u):
                job = i * 2 + u
                T = ps[:, 6, 0:128].rearrange("p (q c) -> p q c", c=32)
                dve.wait_ge(osum_rdy, job + 1)
                dve.tensor_scalar(s4[:, u % 2, :], T[:, :, HD], 1.0 + 1e-8, None, ALU.mult).then_inc(s4_rdy, 1)
                dve.wait_ge(s4_rdy, job + 1)
                dve.reciprocal(r4[:, u % 2, :], s4[:, u % 2, :]).then_inc(r4_rdy, 1)
                dve.wait_ge(r4_rdy, job + 1)
                o = cx[:, :, bass.ds(job, 1), :].rearrange("p s o (h r) -> p h (s o) r", h=2)
                dve.tensor_tensor(o, T[:, :, 0:HD].rearrange("p (h s) r -> p h s r", h=2),
                                  r4[:, u % 2, :].rearrange("p (h s) -> p h s", h=2).unsqueeze(3).broadcast_to([P, 2, 2, HD]), ALU.mult).then_inc(cx_rdy, 1)

            def step(i, x):
                if alive(i, x, IT):
                    clip(i, x)
                if (x - EVAC_LAG) % NCH == 0 and alive(i, (x - EVAC_LAG) // NCH, 2):
                    evac(i, (x - EVAC_LAG) // NCH)
                if (x - NORM_LAG) % NCH == 0 and alive(i, (x - NORM_LAG) // NCH, 2):
                    norm(i, (x - NORM_LAG) // NCH)
                y = x - LO_LAG
                if alive(i, y, IT):
                    low(i, y)

            for x in range(IT):
                step(0, x)
            with dve.Fori(1, NJ // 2 - 1) as i:
                for x in range(IT):
                    step(i, x)
            for x in range(DRAIN):
                step(NJ // 2 - 1, x)
                if x < NT:
                    dve.tensor_tensor(resid[:, x, :], resid[:, x, :], bet[:], ALU.add).then_inc(beta_rdy, 1)
            dve.wait_ge(beta_rdy, NT)
            for q in range(4):
                dve.wait_ge(cTh_rdy, q + 1)
                dve.tensor_tensor(cTxl[:, q, :], ps[:, q, :], cTxh[:, q, :].bitcast(F32), ALU.subtract).then_inc(cTl_rdy, 1)
            for q in range(4):
                dve.wait_ge(dl_rdy, q + 1)
                dve.scalar_tensor_tensor(out=dlt[:, 2 * q:2 * q + 2, :], in0=ps[:, 4 + q, :].rearrange("p (t d) -> p t d", t=2), scalar=rs[:],
                                         in1=bo[:].unsqueeze(1).broadcast_to([P, 2, D]), op0=ALU.mult, op1=ALU.add).then_inc(dl_a, 1)
            dve.wait_ge(dl_a, 4)
            for t in range(NT):
                dve.bn_stats(st6[:, t, :], dlt[:, t, :]).then_inc(dl_a, 1)
            dve.wait_ge(dl_a, 4 + NT)
            for t in range(NT):
                dve.bn_aggr(mv[:, t, :], st6[:, t, :]).then_inc(dl_a, 1)
            dve.wait_ge(dl_a, DLA)
            for t in range(NT):
                dve.scalar_tensor_tensor(out=dlt[:, t, :], in0=dlt[:, t, :], scalar=mv[:, t, 0:1], in1=gam[:], op0=ALU.subtract, op1=ALU.mult).then_inc(dl_b, 1)
            dve.wait_ge(dl_std, 1)
            dve.reciprocal(rstd[:], std[:]).then_inc(dl_b, 1)
            dve.wait_ge(dl_b, NT + 1)
            for t in range(NT):
                dve.scalar_tensor_tensor(out=resid[:, t, :], in0=dlt[:, t, :], scalar=rstd[:, t:t + 1], in1=resid[:, t, :], op0=ALU.mult, op1=ALU.add).then_inc(dl_b, 1)
            dve.wait_ge(dl_b, 2 * NT + 1)
            if stop == "C":
                dve.sem_inc(out_go, 1)
                return
            ffn(FFN["D"])
            dve.sem_inc(out_go, 1)


def kernel(**inp):
    import concourse.bacc as bacc
    from concourse.bass_utils import run_bass_kernel_spmd

    get = lambda n: np.ascontiguousarray(inp[n])
    g0, u0, d0 = get("L0_ffn_gate_proj"), get("L0_ffn_up_proj"), get("L0_ffn_down_proj")
    ex0 = [g0.reshape(E * I0, D), u0.reshape(E * I0, D), d0.transpose(0, 2, 1).reshape(E * I0, D)]
    sh0 = [get("L0_ffn_shared_gate_w"), get("L0_ffn_shared_up_w"), get("L0_ffn_shared_down_w").T]
    ex1 = [get("L1_ffn_Wu").transpose(0, 2, 1).reshape(E * I1, D), get("L1_ffn_Wg").transpose(0, 2, 1).reshape(E * I1, D),
           get("L1_ffn_Wd").reshape(E * I1, D)]
    sh1 = [get("L1_ffn_Su")[0].T, get("L1_ffn_Sg")[0].T, get("L1_ffn_Sd")[0]]

    def pack(shared, experts, width):
        pad = -len(shared[0]) % P
        g, u, d = (np.concatenate([np.pad(s, ((0, pad), (0, 0))), e]) for s, e in zip(shared, experts))
        n = len(g) // P
        first = (len(shared[0]) + pad) // P
        sel = np.zeros((n, P, P), np.float32)
        for r in range(E * width):
            sel[first + r // P, r // width, r % P] = sel[first + r // P, 32 + r // width, r % P] = 1.0
        col = lambda w: w.reshape(n, P, KT, P).transpose(0, 3, 2, 1).reshape(n, P, D)
        return np.ascontiguousarray(np.concatenate([col(g), col(u), d.reshape(n, P, D), sel], axis=2))

    c = get("ctx_2048")
    tr = lambda n: np.ascontiguousarray(get(n).T)
    row = np.arange(P)[:, None]
    msum = np.zeros((VC, 2, HD + 1), np.float32)
    for h in range(2):
        for r in range(HD):
            msum[h * HD + r, h, r] = msum[PR + h * HD + r, h, r] = 1.0
        msum[2 * PR, h, HD] = 1.0
    before = lambda w: np.tile(np.tril(np.ones((w, w), np.float32), -1).reshape(1, w * w), (P, 1))
    arrays = {
        "x": get("x").reshape(NB * SEQ, D),
        "ctxT": np.ascontiguousarray(np.pad(c.transpose(0, 2, 1), ((0, 0), (0, 0), (0, MP - M))).reshape(NB * KT, P, MP)),
        "ctxN": np.pad(c, ((0, 0), (0, MT * P - M), (0, 0))),
        "attend": np.pad(get("mask_BxS2_bk0").view(np.uint8), ((0, 0), (0, 4 * MW - M))).view(np.int32),
        "keep": np.pad(get("mask_BxS2_ik0"), ((0, 0), (0, MP - M))),
        "wqT": tr("L1_xattn_Wq"), "wkT": tr("L1_xattn_Wk"), "wvT": tr("L1_xattn_Wv"), "woT": tr("L1_xattn_Wo"),
        "bq": get("L1_xattn_bq").reshape(NPAIR, PR).T, "bk": get("L1_xattn_bk").reshape(KT, P).T, "bv": get("L1_xattn_bv"), "bo": get("L1_xattn_bo"),
        "gam": get("L1_xattn_ln_gamma"), "bet": get("L1_xattn_ln_beta"), "rs": get("L1_xattn_residual_scale").reshape(1),
        "gw0": tr("L0_ffn_gate_weight"), "gb0": get("L0_ffn_e_score_correction_bias"),
        "gw1": tr("L1_ffn_router_w"), "gb1": get("L1_ffn_router_bias"),
        "w0": pack(sh0, ex0, I0), "w1": pack(sh1, ex1, I1),
        "ident": np.eye(P, dtype=np.float32), "tri16": before(E), "tri4": before(4), "msum": msum,
        "hmask": ((row % PR) // HD == np.arange(2)[None, :]).astype(np.float32),
    }
    nc = bacc.Bacc("TRN2", target_bir_lowering=False, num_devices=1)
    sent, a = {}, {}
    for name, v in arrays.items():
        v = np.ascontiguousarray(v)
        sent[f"in_{name}"] = v
        a[name] = nc.dram_tensor(f"in_{name}", v.shape, mybir.dt.from_np(v.dtype), kind="ExternalInput").ap()
    out = nc.dram_tensor("out_0", (NB * SEQ, D), F32, kind="ExternalOutput").ap()
    build(nc, a, out, STOP)
    r = run_bass_kernel_spmd(nc, [sent], core_ids=[0])
    return r.results[0]["out_0"].reshape(NB, SEQ, D)


STOP = "D"
```
